# Optimizing a Trainium2 kernel written in Bass

```python
import numpy as np
import jax
import jax.numpy as jnp

def _softmax(x, axis=-1):
    return jax.nn.softmax(x, axis=axis)

def _gelu(x):
    return jax.nn.gelu(x, approximate=True)

def _silu(x):
    return jax.nn.silu(x)

def _sigmoid(x):
    return jax.nn.sigmoid(x)

def _layernorm(x, axis=-1, eps=1e-05):
    m = jnp.mean(x, axis=axis, keepdims=True)
    v = jnp.var(x, axis=axis, keepdims=True)
    return (x - m) / jnp.sqrt(v + eps)

def _scatter_add(tgt, idx, src, axis=0):
    return tgt.at[idx].add(src)

def _segment_sum(src, seg, n):
    return jax.ops.segment_sum(src, seg, n)
kernel_name = 'mk_adj_resnorm_d4_adj_r2_037baf'

def setup_inputs(seed: int=0):
    np.random.seed(seed)
    _w = jnp.asarray

    def _rec_inputs():
        import jax
        import jax.numpy as jnp
        _gk = jax.random.key(seed)
        x = -0.000929 + 1 * jax.random.normal(jax.random.fold_in(_gk, 1), (4096, 128), jnp.float32)
        _a = jax.random.bernoulli(jax.random.fold_in(_gk, 2), 0.00390625, (4096, 4096))
        _a = jnp.logical_or(_a, jnp.swapaxes(_a, -1, -2))
        _a = jnp.logical_or(_a, jnp.eye(4096, dtype=bool))
        _af = _a.astype(jnp.float32)
        _af = _af * jax.random.uniform(jax.random.fold_in(_gk, 3), (4096, 4096), jnp.float32, 0.05, 5.41998)
        adj = _af
        return (x, adj)
    x, adj = _rec_inputs()

    def _L0_gnn_setup():
        import jax, jax.numpy as jnp
        import numpy as np
        IN_F, OUT_F = (128, 128)
        R, LEV, N = (2, 2, 4096)
        JD = (R - 1) * LEV + 1
        key = jax.random.key(seed)
        ks = jax.random.split(key, 7)
        x = jax.random.normal(ks[0], (N, IN_F), dtype=jnp.float32)
        d_list = jax.random.uniform(ks[1], (JD, N), dtype=jnp.float32)
        U = jax.random.normal(ks[2], (N, N), dtype=jnp.float32)
        Vt = jax.random.normal(ks[3], (N, N), dtype=jnp.float32)
        bound = float(np.sqrt(6.0 / (IN_F + OUT_F)))
        weight = jax.random.uniform(ks[4], (IN_F, OUT_F), dtype=jnp.float32, minval=-bound, maxval=bound)
        filt = jax.random.uniform(ks[5], (JD, N), dtype=jnp.float32, minval=0.9, maxval=1.1)
        bias = jnp.zeros((OUT_F,), dtype=jnp.float32)
        return {'x': x, 'd_list': d_list, 'U': U, 'Vt': Vt, 'weight': weight, 'filt': filt, 'bias': bias}
    _L0_gnn_all = _L0_gnn_setup()
    _L0_gnn_in = {k: v for k, v in _L0_gnn_all.items() if k in ('d_list', 'weight', 'filt', 'bias')}
    del _L0_gnn_all

    def _L1_gnn_setup():
        import jax, jax.numpy as jnp
        import numpy as np
        N = 4096
        H = 128
        key = jax.random.key(seed)
        k_x, k_A, k_W = jax.random.split(key, 3)
        x = jax.random.normal(k_x, (N, H), dtype=jnp.float32)
        A = jax.random.uniform(k_A, (N, N), dtype=jnp.float32)
        alpha = jnp.array([0.5], dtype=jnp.float32)
        bound = 1.0 / np.sqrt(H)
        W = jax.random.uniform(k_W, (H, H), dtype=jnp.float32, minval=-bound, maxval=bound)
        b = jnp.zeros((H,), dtype=jnp.float32)
        t = jnp.zeros((1,), dtype=jnp.float32)
        return {'t': t, 'x': x, 'A': A, 'alpha': alpha, 'W': W, 'b': b}
    _L1_gnn_all = _L1_gnn_setup()
    _L1_gnn_in = {k: v for k, v in _L1_gnn_all.items() if k in ('t', 'alpha', 'W', 'b')}
    del _L1_gnn_all

    def _L2_gnn_setup():
        import jax, jax.numpy as jnp
        import numpy as np

        def _lap_mul(A, x):
            d = 1.0 / jnp.sqrt(jnp.sum(A, axis=-1))
            return d[:, None] * (A @ (d[:, None] * x))
        key = jax.random.key(seed)
        k1, k2, k3, k4, k5, k6 = jax.random.split(key, 6)
        N, D_IN, D_OUT = (2048, 128, 128)
        x = jax.random.normal(k1, (N, D_IN), dtype=jnp.float32)
        A = jax.random.uniform(k2, (N, N), dtype=jnp.float32)
        s1 = 1.0 / np.sqrt(D_IN)
        W1 = jax.random.uniform(k3, (D_IN, D_OUT), minval=-s1, maxval=s1, dtype=jnp.float32)
        b1 = jax.random.uniform(k4, (D_OUT,), minval=-s1, maxval=s1, dtype=jnp.float32)
        W2 = jax.random.uniform(k5, (D_IN, D_OUT), minval=-s1, maxval=s1, dtype=jnp.float32)
        b2 = jax.random.uniform(k6, (D_OUT,), minval=-s1, maxval=s1, dtype=jnp.float32)
        return {'x': x, 'A': A, 'W1': W1, 'b1': b1, 'W2': W2, 'b2': b2, 'sigma': 1, 'k': 4}
    _L2_gnn_all = _L2_gnn_setup()
    _L2_gnn_in = {k: v for k, v in _L2_gnn_all.items() if k in ('W1', 'b1', 'W2', 'b2')}
    del _L2_gnn_all

    def _L3_gnn_setup():
        import jax, jax.numpy as jnp
        import numpy as np
        IN_DIM = 128
        OUT_DIM = 128
        N = 8192
        key = jax.random.key(seed)
        k_x, k_adj, k_w, k_b = jax.random.split(key, 4)
        x = jax.random.normal(k_x, (N, IN_DIM), dtype=jnp.float32)
        adj = jax.random.uniform(k_adj, (N, N), dtype=jnp.float32)
        bound = 1.0 / np.sqrt(2 * IN_DIM)
        W = jax.random.uniform(k_w, (OUT_DIM, 2 * IN_DIM), dtype=jnp.float32, minval=-bound, maxval=bound)
        b = jax.random.uniform(k_b, (OUT_DIM,), dtype=jnp.float32, minval=-bound, maxval=bound)
        return {'x': x, 'adj': adj, 'W': W, 'b': b}
    _L3_gnn_all = _L3_gnn_setup()
    _L3_gnn_in = {k: v for k, v in _L3_gnn_all.items() if k in ('W', 'b')}
    del _L3_gnn_all
    return {'x': x, 'adj': adj, 'L0_gnn_d_list': _L0_gnn_in['d_list'], 'L0_gnn_weight': _L0_gnn_in['weight'], 'L0_gnn_filt': _L0_gnn_in['filt'], 'L0_gnn_bias': _L0_gnn_in['bias'], 'L1_gnn_t': _L1_gnn_in['t'], 'L1_gnn_alpha': _L1_gnn_in['alpha'], 'L1_gnn_W': _L1_gnn_in['W'], 'L1_gnn_b': _L1_gnn_in['b'], 'L2_gnn_W1': _L2_gnn_in['W1'], 'L2_gnn_b1': _L2_gnn_in['b1'], 'L2_gnn_W2': _L2_gnn_in['W2'], 'L2_gnn_b2': _L2_gnn_in['b2'], 'L3_gnn_W': _L3_gnn_in['W'], 'L3_gnn_b': _L3_gnn_in['b']}

def reference(x, adj, L0_gnn_d_list, L0_gnn_weight, L0_gnn_filt, L0_gnn_bias, L1_gnn_t, L1_gnn_alpha, L1_gnn_W, L1_gnn_b, L2_gnn_W1, L2_gnn_b1, L2_gnn_W2, L2_gnn_b2, L3_gnn_W, L3_gnn_b):
    import jax
    import jax.numpy as jnp

    def _L0_gnn_ref(x, d_list, U, Vt, weight, filt, bias):
        import jax, jax.numpy as jnp
        import numpy as np
        IN_F, OUT_F = (128, 128)
        R, LEV, N = (2, 2, 4096)
        JD = (R - 1) * LEV + 1
        xw = x @ weight
        Vxw = Vt @ xw
        scale = jnp.sum(d_list * filt * d_list, axis=0)
        out = U @ (scale[:, None] * Vxw)
        return out + bias

    def _L1_gnn_ref(t, x, A, alpha, W, b):
        import jax, jax.numpy as jnp
        import numpy as np
        N = 4096
        H = 128
        a = alpha[0]
        A_prime = a * A
        diag = jnp.diagonal(A_prime) + (1.0 - a)
        A_prime = A_prime.at[jnp.arange(N), jnp.arange(N)].set(diag)
        out_degree = A_prime.sum(axis=1)
        inv_deg = jnp.where(out_degree == 0.0, 0.0, 1.0 / out_degree)
        x = inv_deg[:, None] * A_prime @ x
        x = x @ W.T + b
        return jax.nn.relu(x)

    def _L2_gnn_ref(x, A, W1, b1, W2, b2, sigma, k):
        import jax, jax.numpy as jnp
        import numpy as np

        def _lap_mul(A, x):
            d = 1.0 / jnp.sqrt(jnp.sum(A, axis=-1))
            return d[:, None] * (A @ (d[:, None] * x))
        z = _lap_mul(A, x) @ W1 + b1
        z = jax.nn.leaky_relu(z, negative_slope=0.1)
        sq = jnp.sum(z * z, axis=-1)
        d2 = sq[:, None] + sq[None, :] - 2.0 * (z @ z.T)
        d2 = jnp.maximum(d2, 0.0)
        S = jnp.sqrt(d2 + 1e-10)
        S = jnp.exp(-S / (2.0 * sigma))
        order = jnp.argsort(-S, axis=-1)
        ranks = jnp.argsort(order, axis=-1)
        S = jnp.where(ranks < k, S, 0.0)
        A2 = S + A
        out = _lap_mul(A2, x) @ W2 + b2
        return out

    def _L3_gnn_ref(x, adj, W, b):
        import jax, jax.numpy as jnp
        import numpy as np
        IN_DIM = 128
        OUT_DIM = 128
        N = 8192
        h_N = jnp.matmul(adj, x)
        h_cat = jnp.concatenate([x, h_N], axis=-1)
        out = jnp.maximum(jnp.einsum('nd,od->no', h_cat, W) + b, 0.0)
        return out
    x = _layernorm(x + _L0_gnn_ref(x, L0_gnn_d_list, adj, adj, L0_gnn_weight, L0_gnn_filt, L0_gnn_bias), axis=-1)
    x = _layernorm(x + _L1_gnn_ref(L1_gnn_t, x, adj, L1_gnn_alpha, L1_gnn_W, L1_gnn_b), axis=-1)
    x = _layernorm(x + _L2_gnn_ref(x, adj, L2_gnn_W1, L2_gnn_b1, L2_gnn_W2, L2_gnn_b2, 1, 4), axis=-1)
    x = _layernorm(x + _L3_gnn_ref(x, adj, L3_gnn_W, L3_gnn_b), axis=-1)
    return x

_drawn_inputs = setup_inputs


def setup_inputs(seed=0):
    import zlib

    import numpy as np

    out = dict(_drawn_inputs(seed))
    spreads = {'L0_gnn_bias': (0.0, 0.8), 'L1_gnn_b': (0.0, 0.1)}
    factors = {'L2_gnn_W1': 8.0, 'L2_gnn_b1': 8.0, 'L3_gnn_b': 8.0}
    for name, (base, spread) in spreads.items():
        noise = np.random.default_rng([zlib.crc32(name.encode()), seed]).standard_normal(out[name].shape)
        drawn = base * np.exp(spread * noise) if base else spread * noise
        out[name] = jnp.asarray(drawn.astype(out[name].dtype))
    for name, factor in factors.items():
        out[name] = (out[name] * factor).astype(out[name].dtype)
    return out
```

```python
from contextlib import ExitStack

import concourse.bass as bass
from concourse import mybir

F32 = mybir.dt.float32
F16 = mybir.dt.float16
BF16 = mybir.dt.bfloat16
U32 = mybir.dt.uint32
ALU = mybir.AluOpType
ACT = mybir.ActivationFunctionType
AXX = mybir.AxisListType.X

P = 128
CHUNK = 512
TPC = CHUNK // P
KEPT = 7
UNIT = 5
LAG = 3
TOP = 4
LAST = 5

A_SCALE = 64.0
Z_SCALE = 16.0
Y_SCALE = {-1: 256.0, 0: 16.0, 1: 128.0, 2: 512.0, 3: 512.0, 4: 128.0}
OPERAND = [0, 1, 0, 1, 1, 0]


def gnn_kernel(nc, x, adj, d_list, w0, filt, bias0, alpha, w1, b1, wz, bz, w2, b2, w3, b3, out):
    N, D = x.shape
    JD = d_list.shape[0]
    KT = N // P
    NCH = N // CHUNK
    NAT_UNITS = KT // TPC
    UPC = (KT - KEPT) // UNIT
    assert D == P and UPC * UNIT + KEPT == KT and NCH % 2 == 0

    at_dram = nc.dram_tensor("at_scratch", [NCH, UPC, P, UNIT * 2 * CHUNK], F16).ap()
    x_dram = [None, nc.dram_tensor("x1_scratch", [N, D], F32).ap(), nc.dram_tensor("x2_scratch", [N, D], F32).ap(),
              nc.dram_tensor("x3_scratch", [N, D], F32).ap()]
    x_dram[0] = x
    y_dram = nc.dram_tensor("y_scratch", [N, D], F32).ap()

    with ExitStack() as ctx:
        def sb(name, shape, dt):
            return ctx.enter_context(nc.sbuf_tensor(name, shape, dt))

        def ps(name, shape, dt=F32):
            return ctx.enter_context(nc.psum_tensor(name, shape, dt))

        def sem(name):
            return ctx.enter_context(nc.semaphore(name))

        kept = sb("kept", [P, NCH, KEPT, 2, CHUNK], F16)
        slot_elems = UNIT * 2 * CHUNK
        nat_elems = TPC * CHUNK * 2
        region = sb("region", [P, 4 * nat_elems + 2 * slot_elems], F16)
        ring = [region[:, s * slot_elems:(s + 1) * slot_elems].rearrange("p (k h n) -> p k h n", k=UNIT, h=2)
                for s in range(UPC)]
        nat = [region[:, s * nat_elems:(s + 1) * nat_elems].bitcast(F32).rearrange("p (t k) -> p t k", t=TPC)
               for s in range(4)]
        stage_flat = [region[:, 4 * nat_elems + s * slot_elems:4 * nat_elems + (s + 1) * slot_elems] for s in range(2)]
        stage = [s.rearrange("p (k h n) -> p k h n", k=UNIT, h=2) for s in stage_flat]
        x0 = region[:, 4 * nat_elems:4 * nat_elems + 2 * KT * D].bitcast(F32).rearrange("p (t f) -> p t f", t=KT)
        near = [region[:, s * 2 * N:(s + 1) * 2 * N].bitcast(F32) for s in range(2)]
        sqT = region[:, 4 * nat_elems:4 * nat_elems + N].bitcast(BF16)

        yop = [sb(f"yop{b}", [P, 2, KT, D], F16) for b in range(2)]
        zT = yop[0][:, :, :, :].rearrange("p h t f -> p h (t f)")
        hT = sb("hT", [P, CHUNK], F32)
        xT = sb("xT", [P, CHUNK], F32)
        t_nat = sb("t_nat", [P, TPC, D], F32)
        xin = sb("xin", [P, TPC, D], F32)
        xout = sb("xout", [P, TPC, D], F32)
        gath = [sb(f"gath{b}", [P, TPC, D], F32) for b in range(2)]
        ident = sb("ident", [P, P], F32)
        ident16 = sb("ident16", [P, P], BF16)
        w0_sb, wz_sb, w2_sb = (sb(n, [D, D], F32) for n in ("w0_sb", "wz_sb", "w2_sb"))
        wT = sb("wT", [D, 3, D], F32)
        bias = {k: sb(f"bias{k}", [P, D], F32) for k in (1, 2, 3, 4, 5)}
        alpha_c = sb("alpha_c", [P, 1], F32)
        alpha_acc = sb("alpha_acc", [P, 1], F32)
        one_alpha = sb("one_alpha", [P, 1], F32)
        eps_ln = sb("eps_ln", [P, 1], F32)
        eps_d2 = sb("eps_d2", [P, 1], F32)
        scale = sb("scale", [P, KT], F32)
        rs_part = [sb(f"rs_part{b}", [P, NAT_UNITS, TPC], F32) for b in range(2)]
        rs = sb("rs", [P, KT], F32)
        inv_deg = sb("inv_deg", [P, KT], F32)
        zero_deg = sb("zero_deg", [P, KT], F32)
        dinv = sb("dinv", [P, KT], F32)
        dinv2 = sb("dinv2", [P, KT], F32)
        droot = sb("droot", [P, KT], F32)
        stats = sb("stats", [P, TPC, 6], F32)
        mv = sb("mv", [P, TPC, 2], F32)
        std = sb("std", [P, TPC], F32)
        rstd = sb("rstd", [P, TPC], F32)
        sq = sb("sq", [P, KT], F32)
        sq_rest = sb("sq_rest", [P, KT], F32)
        sq_parts = sb("sq_parts", [P, KT, 3], BF16)
        ones3 = sb("ones3", [P, P], BF16)
        top8 = [sb(f"top8_{b}", [P, 8], F32) for b in range(2)]
        idx8 = [sb(f"idx8_{b}", [P, 8], U32) for b in range(2)]
        S = sb("S", [P, KT, TOP], F32)
        idx = sb("idx", [P, KT, TOP], U32)
        idx_chunk = sb("idx_chunk", [P, TPC, TOP], U32)

        acc = [ps(f"acc{b}", [P, CHUNK]) for b in range(2)]
        pt = [ps(f"pt{b}", [P, CHUNK]) for b in range(4)]
        pnat = ps("pnat", [P, TPC, D])
        pxT = ps("pxT", [P, CHUNK])


        def sq_bank(c):
            return acc[c % 2][:, :].bitcast(BF16)[0:3, 0:CHUNK]

        x0_loaded, par_loaded, consts, ident_made = sem("x0_loaded"), sem("par_loaded"), sem("consts"), sem("ident_made")
        y0_ready = sem("y0_ready")
        setup_pe, setup_dve = sem("setup_pe"), sem("setup_dve")
        nat_loaded = [sem(f"nat_loaded{s}") for s in range(4)]
        rows_summed_act, rows_summed_dve = sem("rows_summed_act"), sem("rows_summed_dve")
        tr_done, high_done, low_done = sem("tr_done"), sem("high_done"), sem("low_done")
        stage_used = sem("stage_used")
        stage_stored = [sem(f"stage_stored{s}") for s in range(2)]
        unit_loaded = [sem(f"unit_loaded{s}") for s in range(UPC)]
        unit_used = sem("unit_used")
        acc_full, hT_ready, nat_full, nat_read = sem("acc_full"), sem("hT_ready"), sem("nat_full"), sem("nat_read")
        xT_full, xT_ready, zT_read = sem("xT_full"), sem("xT_ready"), sem("zT_read")
        xin_loaded, xin_free = sem("xin_loaded"), sem("xin_free")
        var_ready, std_ready, yop_ready = sem("var_ready"), sem("std_ready"), sem("yop_ready")
        xout_ready, xout_stored = sem("xout_ready"), sem("xout_stored")
        z_ready = sem("z_ready")
        chain_dve, rows_closed = sem("chain_dve"), sem("rows_closed")
        sq_ready, sqT_full, sqT_ready = sem("sq_ready"), sem("sqT_full"), sem("sqT_ready")
        near_full, near_copied, near_used = sem("near_full"), sem("near_copied"), sem("near_used")
        d2_ready, S_ready, deg_ready, root_ready = sem("d2_ready"), sem("S_ready"), sem("deg_ready"), sem("root_ready")
        idx_ready, idx_used, gath_used = sem("idx_ready"), sem("idx_used"), sem("gath_used")
        gath_loaded = [sem(f"gath_loaded{b}") for b in range(2)]
        mix_ready = sem("mix_ready")

        def nth(passes, p, c):
            return passes.index(p) * NCH + c + 1

        ALL = [0, 1, 2, 3, 4, 5]
        XT = [2, 3, 4, 5]
        XTS = [2, 4, 5]
        XIN = [1, 2, "y", 4, 5]
        LN = [1, 2, 4, 5]
        XOUT = [1, 2, "y", 4, 5]
        YOP = [0, 1, 2, "y", 4]

        def each_chunk(eng, body):
            body(0, 0, 0)
            body(1, 1, 0)
            with eng.Fori(1, NCH // 2) as pair:
                body(pair * 2, 0, pair)
                body(pair * 2 + 1, 1, pair)

        def rows(t, c):
            return t[bass.ds(c * CHUNK, CHUNK), :].rearrange("(t p) f -> p t f", p=P)

        def per_row(v, c):
            return v[:, bass.ds(c * TPC, TPC)].unsqueeze(2).to_broadcast([P, TPC, D])

        def over_tiles(v):
            return v[:, :].unsqueeze(1).to_broadcast([P, TPC, D])

        block = ctx.enter_context(nc.Block())

        @block.sync
        def _(sp):
            sp.dma_start(x0, x.rearrange("(t p) f -> p t f", p=P)).then_inc(x0_loaded, 16)

            def load_natural(c, par, m):
                for u in range(NAT_UNITS):
                    s = u % 4
                    if not (isinstance(c, int) and c == 0 and u < 4):
                        before = c * NAT_UNITS + (u - 4) + 1
                        sp.wait_ge(tr_done, before * TPC)
                        sp.nop(nofuse=True)
                        half = c * (NAT_UNITS // 2) + (u - 4) // 2 + 1
                        sp.wait_ge(rows_summed_dve if u % 2 == 0 else rows_summed_act, half)
                    sp.dma_start(nat[s], adj[bass.ds(c * CHUNK, CHUNK), u * CHUNK:(u + 1) * CHUNK]
                                 .rearrange("(t p) k -> p t k", p=P)).then_inc(nat_loaded[s], 16)
            each_chunk(sp, load_natural)

            sp.wait_ge(tr_done, NCH * KT)
            sp.wait_ge(rows_summed_dve, NCH * NAT_UNITS // 2)
            sp.wait_ge(rows_summed_act, NCH * NAT_UNITS // 2)
            sp.wait_ge(stage_used, NCH * UPC)
            for s in range(2):
                sp.wait_ge(stage_stored[s], 16 * NCH * UPC // 2)

            def stream(p):
                def units(c, par, m):
                    for u in range(UPC):
                        if p > 1 or not isinstance(c, int) or c > 0:
                            sp.wait_ge(unit_used, (p - 1) * NCH * UPC + c * UPC + u - UPC + 1)
                        sp.dma_start(ring[u].rearrange("p k h n -> p (k h n)"),
                                     at_dram[bass.ds(c, 1), u, :, :].rearrange("c p n -> (c p) n")
                                     ).then_inc(unit_loaded[u], 16)
                each_chunk(sp, units)

            stream(1)
            stream(2)
            stream(3)
            sp.wait_ge(near_used, KT)
            stream(4)
            stream(5)

        @block.gpsimd
        def _(pool):
            pool.memset(ident[:, :], 0.0).then_inc(ident_made, 1)
            pool.memset(ones3[:, :], 0.0).then_inc(ident_made, 1)
            pool.memset(eps_ln[:, :], 1e-5).then_inc(consts, 1)
            pool.memset(eps_d2[:, :], 1e-10).then_inc(consts, 1)
            pool.wait_ge(ident_made, 2)
            pool.memset(ones3[0:3, :], 1.0).then_inc(consts, 1)
            pool.affine_select(out=ident[:, :], in_=ident[:, :], compare_op=ALU.not_equal, fill=1.0, base=0,
                               pattern=[[-1, P]], channel_multiplier=1).then_inc(ident_made, 1)
            n = 0
            for dst, src in [(t_nat[:, 0, :], w1), (t_nat[:, 1:3, :], w3.rearrange("o (h f) -> o h f", h=2)),
                             (hT[0:JD * KT, 0:P], d_list.rearrange("j (t p) -> (j t) p", p=P)),
                             (hT[0:JD * KT, P:2 * P], filt.rearrange("j (t p) -> (j t) p", p=P)),
                             (w0_sb[:, :], w0), (wz_sb[:, :], wz), (w2_sb[:, :], w2),
                             (bias[1][:, :], bias0.partition_broadcast(P)), (bias[2][:, :], b1.partition_broadcast(P)),
                             (bias[3][:, :], bz.partition_broadcast(P)), (bias[4][:, :], b2.partition_broadcast(P)),
                             (bias[5][:, :], b3.partition_broadcast(P)), (alpha_c[:, :], alpha.partition_broadcast(P))]:
                pool.dma_start(dst, src).then_inc(par_loaded, 16)
                n += 1
            assert n == PARAMS

            def store_units(c, par, m):
                for u in range(UPC):
                    s = (par * UPC + u) % 2
                    pool.wait_ge(low_done, c * KT + KEPT + (u + 1) * UNIT)
                    pool.nop(nofuse=True)
                    pool.dma_start(at_dram[bass.ds(c, 1), u, :, :].rearrange("c p n -> (c p) n"),
                                   stage_flat[s]).then_inc(stage_stored[s], 16)
            each_chunk(pool, store_units)

            def load_xin(p, source, c, first):
                if not first:
                    pool.wait_ge(xin_free, nth(XIN, p, c) - 1)
                pool.nop(nofuse=True)
                pool.dma_start(xin[:, :, :], rows(source, c)).then_inc(xin_loaded, 16)

            def store_xout(p, target, c):
                pool.wait_ge(xout_ready, nth(XOUT, p, c))
                pool.nop(nofuse=True)
                pool.dma_start(rows(target, c), xout[:, :, :]).then_inc(xout_stored, 16)

            def residual_pass(p, source, target):
                def body(c, par, m):
                    load_xin(p, source, c, p == 1 and isinstance(c, int) and c == 0)
                    store_xout(p, target, c)
                each_chunk(pool, body)
                pool.wait_ge(xout_stored, 16 * nth(XOUT, p, NCH - 1))

            residual_pass(1, x_dram[0], x_dram[1])
            residual_pass(2, x_dram[1], x_dram[2])
            pool.wait_ge(zT_read, NCH)
            residual_pass("y", x_dram[2], y_dram)

            def gather_pass(c, par, m):
                load_xin(4, x_dram[2], c, False)
                pool.wait_ge(idx_ready, c + 1)
                for r in range(TOP):
                    if not (isinstance(c, int) and c == 0 and r < 2):
                        pool.wait_ge(gath_used, c * TOP + r - 1)
                    pool.nop(nofuse=True)
                    for t in range(TPC):
                        pool.indirect_dma_start(gath[r % 2][:, t, :], None, y_dram,
                                                bass.IndirectOffsetOnAxis(ap=idx_chunk[:, t, r:r + 1], axis=0)
                                                ).then_inc(gath_loaded[r % 2], 16)
                store_xout(4, x_dram[3], c)
            each_chunk(pool, gather_pass)
            pool.wait_ge(xout_stored, 16 * nth(XOUT, 4, NCH - 1))

            residual_pass(5, x_dram[3], out)

        def act_epilogue(act, p, c, par):
            n = nth(ALL, p, c)
            if p in (2, 4, 5):
                act.wait_ge(xT_full, nth(XT, p, c))
                if not (p == 2 and isinstance(c, int) and c == 0):
                    act.wait_ge(nat_full, n - 1)
                    act.wait_ge(hT_ready, n - 1)
                nc.scalar.activation(xT[:, :], pxT[:, :], ACT.Copy,
                                     scale=one_alpha[:, 0:1] if p == 2 else 1.0).then_inc(xT_ready, 1)
            if p in (0, 1, 3, 5):
                act.wait_ge(acc_full, n)
                if not (p == 0 and isinstance(c, int) and c == 0):
                    act.wait_ge(nat_full, n - 1)
                nc.scalar.activation(hT[:, :], acc[par][:, :], ACT.Copy,
                                     scale=1.0 / (A_SCALE * Y_SCALE[p - 1])).then_inc(hT_ready, 1)
            if p in LN:
                act.wait_ge(var_ready, nth(LN, p, c))
                nc.scalar.activation(std[:, :], mv[:, :, 1], ACT.Sqrt, bias=eps_ln[:, 0:1]).then_inc(std_ready, 1)

        @block.scalar
        def _(act):
            act.wait_ge(consts, 3)
            act.wait_ge(y0_ready, 1)
            act.wait_ge(setup_dve, SETUP_DVE)

            def split_high(c, par, m):
                for kt in range(KT):
                    g = c * KT + kt
                    act.wait_ge(tr_done, g + 1)
                    if kt < KEPT:
                        dst = kept[:, bass.ds(c, 1), kt, 0, :].rearrange("p c n -> p (c n)")
                    else:
                        u = (kt - KEPT) // UNIT
                        s = (par * UPC + u) % 2
                        if (kt - KEPT) % UNIT == 0 and not (isinstance(c, int) and c * UPC + u < 2):
                            before = c * UPC + u - 1
                            act.wait_ge(stage_used, before)
                            act.wait_ge(stage_stored[s], 16 * (m * UPC + (par * UPC + u) // 2))
                        dst = stage[s][:, (kt - KEPT) % UNIT, 0, :]
                    nc.scalar.activation(dst, pt[kt % 4][:, :], ACT.Copy, scale=A_SCALE).then_inc(high_done, 1)
                    if kt % 8 == 6:
                        u = kt // TPC
                        act.wait_ge(nat_loaded[u % 4], 16 * (c * 2 + u // 4 + 1))
                        if u == 1 and not (isinstance(c, int) and c < 2):
                            act.wait_ge(rows_closed, c - 1)
                        if not (isinstance(c, int) and c == 0 and u == 1):
                            act.wait_ge(rows_summed_act, c * (NAT_UNITS // 2) + u // 2)
                        for t in range(TPC):
                            discard = (xin, xout)[t // 2][:, :, :].rearrange("p t f -> p (t f)").bitcast(BF16)
                            last = nc.scalar.activation(discard[:, (t % 2) * CHUNK:(t % 2 + 1) * CHUNK],
                                                        nat[u % 4][:, t, :], ACT.Copy,
                                                        accum_out=rs_part[par][:, u, t:t + 1])
                        last.then_inc(rows_summed_act, 1)
                    if kt == 8 and not (isinstance(c, int) and c == 0):
                        act_epilogue(act, 0, c - 1, 1 - par)
            each_chunk(act, split_high)
            act_epilogue(act, 0, NCH - 1, 1)
            act.wait_ge(deg_ready, 1)
            nc.scalar.activation(droot[:, :], rs[:, :], ACT.Sqrt).then_inc(root_ready, 1)

            for p in (1, 2, 3):
                each_chunk(act, lambda c, par, m, p=p: act_epilogue(act, p, c, par))

            for c in range(NCH):
                act.wait_ge(sqT_full, c + 1)
                nc.scalar.activation(sqT[0:3, c * CHUNK:(c + 1) * CHUNK], sq_bank(c), ACT.Copy).then_inc(sqT_ready, 1)

            def copy_near(i, par):
                if not (isinstance(i, int) and i < 2):
                    act.wait_ge(near_used, i - 1)
                for j in range(NCH):
                    act.wait_ge(near_full, i * NCH + j + 1)
                    nc.scalar.activation(near[par][:, j * CHUNK:(j + 1) * CHUNK], pt[j % 4][:, :],
                                         ACT.Copy).then_inc(near_copied, 1)
            copy_near(0, 0)
            copy_near(1, 1)
            with act.Fori(1, KT // 2) as pair:
                copy_near(pair * 2, 0)
                copy_near(pair * 2 + 1, 1)

            act.wait_ge(d2_ready, 1)
            nc.scalar.activation(S[:, :, :], S[:, :, :], ACT.Sqrt, bias=eps_d2[:, 0:1]).then_inc(S_ready, 1)
            act.wait_ge(S_ready, 1)
            nc.scalar.activation(S[:, :, :], S[:, :, :], ACT.Exp, scale=-0.5).then_inc(S_ready, 1)
            act.wait_ge(deg_ready, 2)
            nc.scalar.activation(droot[:, :], droot[:, :], ACT.Sqrt).then_inc(root_ready, 1)

            for p in (4, 5):
                each_chunk(act, lambda c, par, m, p=p: act_epilogue(act, p, c, par))

        @block.vector
        def _(dve):
            count = [0]

            def step(ins):
                count[0] = count[0] + 1
                ins.then_inc(chain_dve, 1)
                dve.wait_ge(chain_dve, count[0])

            steps_of = {}
            start_of = {}

            def counted(kind, c, body):
                if isinstance(c, int) and c == 0:
                    start_of[kind] = count[0]
                else:
                    count[0] = c * steps_of[kind] + start_of[kind]
                before = count[0]
                body()
                if isinstance(c, int) and c == 0:
                    steps_of[kind] = count[0] - before

            def close(kind, chunks=NCH):
                count[0] = start_of[kind] + chunks * steps_of[kind]

            def split(p, src, c):
                k = 3 if p == "y" else p
                buf = yop[OPERAND[k + 1]]
                hi, lo = buf[:, 0, bass.ds(c * TPC, TPC), :], buf[:, 1, bass.ds(c * TPC, TPC), :]
                step(nc.vector.tensor_scalar(hi, src, Y_SCALE[k], None, ALU.mult))
                nc.vector.scalar_tensor_tensor(lo, src, Y_SCALE[k], hi, ALU.mult, ALU.subtract).then_inc(yop_ready, 1)

            def layernorm(p, c):
                for t in range(TPC):
                    last = nc.vector.bn_stats(stats[:, t, :], t_nat[:, t, :])
                step(last)
                dve.nop(nofuse=True)
                for t in range(TPC):
                    last = nc.vector.bn_aggr(mv[:, t, :], stats[:, t, :])
                last.then_inc(var_ready, 1)
                dve.wait_ge(std_ready, nth(LN, p, c))
                step(nc.vector.reciprocal(rstd[:, :], std[:, :]))
                if not (p == 1 and isinstance(c, int) and c == 0):
                    dve.wait_ge(xout_stored, 16 * (nth(XOUT, p, c) - 1))
                for t in range(TPC):
                    last = nc.vector.tensor_scalar(xout[:, t, :], t_nat[:, t, :], mv[:, t, 0:1], rstd[:, t:t + 1],
                                                   ALU.subtract, ALU.mult)
                last.then_inc(xout_ready, 1)
                dve.wait_ge(xout_ready, nth(XOUT, p, c))

            def epilogue(p, c, par):
                n = nth(ALL, p, c)
                if p == 4:
                    step(nc.vector.tensor_copy(idx_chunk[:, :, :], idx[:, bass.ds(c * TPC, TPC), :]))
                    dve.sem_inc(idx_ready, 1)
                    for r in range(TOP):
                        dve.wait_ge(gath_loaded[r % 2], 16 * TPC * (c * 2 + r // 2 + 1))
                        weight = S[:, bass.ds(c * TPC, TPC), r:r + 1].to_broadcast([P, TPC, D])
                        if r == 0:
                            nc.vector.tensor_tensor(t_nat[:, :, :], gath[0][:, :, :], weight, ALU.mult).then_inc(gath_used, 1)
                        else:
                            step(nc.vector.tensor_tensor(gath[r % 2][:, :, :], gath[r % 2][:, :, :], weight, ALU.mult))
                            last = nc.vector.tensor_tensor(t_nat[:, :, :], t_nat[:, :, :], gath[r % 2][:, :, :], ALU.add)
                            last.then_inc(gath_used, 1)
                        dve.wait_ge(gath_used, c * TOP + r + 1)
                    dve.sem_inc(mix_ready, 1)
                if p in (2, 4):
                    dve.wait_ge(xT_ready, nth(XTS, p, c))
                    dve.wait_ge(acc_full, n)
                    dve.wait_ge(nat_full, n - 1)
                    factor = alpha_acc[:, 0:1] if p == 2 else 1.0 / (A_SCALE * Y_SCALE[3])
                    nc.vector.scalar_tensor_tensor(hT[:, :], acc[par][:, :], factor, xT[:, :], ALU.mult,
                                                   ALU.add).then_inc(hT_ready, 1)
                dve.wait_ge(nat_full, n)
                if p == 0:
                    nc.vector.tensor_tensor(t_nat[:, :, :], pnat[:, :, :], per_row(scale, c), ALU.mult).then_inc(nat_read, 1)
                    dve.wait_ge(nat_read, n)
                    split(0, t_nat[:, :, :], c)
                    return
                if p == 1:
                    dve.wait_ge(xin_loaded, 16 * nth(XIN, p, c))
                    nc.vector.tensor_tensor(t_nat[:, :, :], pnat[:, :, :], xin[:, :, :], ALU.add).then_inc(nat_read, 1)
                    dve.wait_ge(nat_read, n)
                    dve.sem_inc(xin_free, 1)
                    step(nc.vector.tensor_tensor(t_nat[:, :, :], t_nat[:, :, :], over_tiles(bias[1]), ALU.add))
                if p in (2, 3, 4):
                    factor = {2: inv_deg, 3: dinv, 4: dinv2}[p]
                    nc.vector.tensor_tensor(t_nat[:, :, :], pnat[:, :, :], per_row(factor, c), ALU.mult).then_inc(nat_read, 1)
                    dve.wait_ge(nat_read, n)
                    step(nc.vector.tensor_tensor(t_nat[:, :, :], t_nat[:, :, :], over_tiles(bias[p]), ALU.add))
                if p == 5:
                    nc.vector.tensor_tensor(t_nat[:, :, :], pnat[:, :, :], over_tiles(bias[5]), ALU.add).then_inc(nat_read, 1)
                    dve.wait_ge(nat_read, n)
                if p in (2, 4, 5):
                    dve.wait_ge(xin_loaded, 16 * nth(XIN, p, c))
                    if p == 4:
                        step(nc.vector.tensor_tensor(t_nat[:, :, :], t_nat[:, :, :], xin[:, :, :], ALU.add))
                    else:
                        step(nc.vector.scalar_tensor_tensor(t_nat[:, :, :], t_nat[:, :, :], 0.0, xin[:, :, :],
                                                            ALU.max, ALU.add))
                    dve.sem_inc(xin_free, 1)
                if p == 3:
                    if isinstance(c, int) and c == 0:
                        dve.wait_ge(xout_stored, 16 * nth(XOUT, 2, NCH - 1))
                    else:
                        dve.wait_ge(xT_full, nth(XT, 3, c) - 1)
                    step(nc.vector.scalar_tensor_tensor(xout[:, :, :], t_nat[:, :, :], 0.1, t_nat[:, :, :],
                                                        ALU.mult, ALU.max))
                    dve.sem_inc(z_ready, 1)
                    step(nc.vector.tensor_tensor(xin[:, :, :], xout[:, :, :], xout[:, :, :], ALU.mult))
                    step(nc.vector.tensor_reduce(sq[:, bass.ds(c * TPC, TPC)], xin[:, :, :], AXX, ALU.add))
                    dve.wait_ge(xT_full, nth(XT, 3, c))
                    zh = zT[:, 0, bass.ds(c * CHUNK, CHUNK)]
                    step(nc.vector.tensor_scalar(zh, pxT[:, :], Z_SCALE, None, ALU.mult))
                    nc.vector.scalar_tensor_tensor(zT[:, 1, bass.ds(c * CHUNK, CHUNK)], pxT[:, :], Z_SCALE, zh,
                                                   ALU.mult, ALU.subtract).then_inc(zT_read, 1)
                    return
                layernorm(p, c)
                if p == 2:
                    step(nc.vector.tensor_tensor(t_nat[:, :, :], xout[:, :, :], per_row(dinv, c), ALU.mult))
                    split(2, t_nat[:, :, :], c)
                elif p != LAST:
                    split(p, xout[:, :, :], c)

            dve.wait_ge(x0_loaded, 16)
            step(nc.vector.tensor_scalar(yop[0][:, 0, :, :], x0, Y_SCALE[-1], None, ALU.mult))
            nc.vector.scalar_tensor_tensor(yop[0][:, 1, :, :], x0, Y_SCALE[-1], yop[0][:, 0, :, :],
                                           ALU.mult, ALU.subtract).then_inc(y0_ready, 1)
            dve.wait_ge(par_loaded, 16 * PARAMS)
            rows_j = JD * KT
            step(nc.vector.tensor_tensor(hT[0:rows_j, P:2 * P], hT[0:rows_j, 0:P], hT[0:rows_j, P:2 * P], ALU.mult))
            step(nc.vector.tensor_tensor(hT[0:rows_j, 0:P], hT[0:rows_j, 0:P], hT[0:rows_j, P:2 * P], ALU.mult))
            dve.sem_inc(setup_dve, 1)
            dve.wait_ge(setup_pe, 1)
            nc.vector.tensor_copy(wT[:, :, :], pt[0][:, 0:3 * D].rearrange("p (w f) -> p w f", w=3)).then_inc(setup_dve, 1)
            dve.wait_ge(setup_pe, 2)
            nc.vector.tensor_reduce(scale[:, :], pt[1][:, 0:rows_j].rearrange("p (j t) -> p t j", j=JD), AXX,
                                    ALU.add).then_inc(setup_dve, 1)
            dve.wait_ge(ident_made, 3)
            nc.vector.tensor_copy(ident16[:, :], ident[:, :]).then_inc(setup_dve, 1)
            nc.vector.tensor_scalar(one_alpha[:, :], alpha_c[:, :], -1.0, 1.0, ALU.mult, ALU.add).then_inc(setup_dve, 1)
            nc.vector.tensor_scalar(alpha_acc[:, :], alpha_c[:, :], 1.0 / (A_SCALE * Y_SCALE[1]), None,
                                    ALU.mult).then_inc(setup_dve, 1)
            dve.wait_ge(setup_dve, SETUP_DVE)

            def split_low(c, par, m):
                for kt in range(KT):
                    g = c * KT + kt
                    dve.wait_ge(high_done, g + 1)
                    if kt < KEPT:
                        hi = kept[:, bass.ds(c, 1), kt, 0, :].rearrange("p c n -> p (c n)")
                        lo = kept[:, bass.ds(c, 1), kt, 1, :].rearrange("p c n -> p (c n)")
                    else:
                        s = (par * UPC + (kt - KEPT) // UNIT) % 2
                        hi, lo = (stage[s][:, (kt - KEPT) % UNIT, h, :] for h in range(2))
                    nc.vector.scalar_tensor_tensor(lo, pt[kt % 4][:, :], A_SCALE, hi, ALU.mult,
                                                   ALU.subtract).then_inc(low_done, 1)
                    if kt % 8 == 2:
                        u = kt // TPC
                        dve.wait_ge(nat_loaded[u % 4], 16 * (c * 2 + u // 4 + 1))
                        nc.vector.tensor_reduce(rs_part[par][:, u, :], nat[u % 4], AXX, ALU.add
                                                ).then_inc(rows_summed_dve, 1)
                    if kt == 16 and not (isinstance(c, int) and c == 0):
                        counted(0, c - 1, lambda: epilogue(0, c - 1, 1 - par))
                dve.wait_ge(rows_summed_dve, (c + 1) * (NAT_UNITS // 2))
                dve.wait_ge(rows_summed_act, (c + 1) * (NAT_UNITS // 2))
                nc.vector.tensor_reduce(rs[:, bass.ds(c * TPC, TPC)], rs_part[par][:, :, :].rearrange("p u t -> p t u"),
                                        AXX, ALU.add).then_inc(rows_closed, 1)
            each_chunk(dve, split_low)
            counted(0, NCH - 1, lambda: epilogue(0, NCH - 1, 1))
            close(0)

            dve.wait_ge(rows_closed, NCH)
            dve.sem_inc(deg_ready, 1)
            step(nc.vector.tensor_scalar(inv_deg[:, :], rs[:, :], alpha_c[:, 0:1], one_alpha[:, 0:1], ALU.mult, ALU.add))
            step(nc.vector.tensor_scalar(zero_deg[:, :], inv_deg[:, :], 0.0, None, ALU.is_equal))
            step(nc.vector.tensor_tensor(inv_deg[:, :], inv_deg[:, :], zero_deg[:, :], ALU.add))
            step(nc.vector.reciprocal(inv_deg[:, :], inv_deg[:, :]))
            step(nc.vector.tensor_scalar(zero_deg[:, :], zero_deg[:, :], -1.0, 1.0, ALU.mult, ALU.add))
            step(nc.vector.tensor_tensor(inv_deg[:, :], inv_deg[:, :], zero_deg[:, :], ALU.mult))
            dve.wait_ge(root_ready, 1)
            step(nc.vector.reciprocal(dinv[:, :], droot[:, :]))

            def epilogues(p):
                each_chunk(dve, lambda c, par, m: counted(p, c, lambda: epilogue(p, c, par)))
                close(p)

            epilogues(1)
            epilogues(2)
            epilogues(3)

            dve.wait_ge(acc_full, nth(ALL, 3, NCH - 1))
            step(nc.vector.memset(sqT.bitcast(F32), 0.0))
            step(nc.vector.tensor_scalar(sq_rest[:, :], sq[:, :], -0.5 * Z_SCALE * Z_SCALE, None, ALU.mult))
            for k in range(3):
                step(nc.vector.tensor_copy(sq_parts[:, :, k], sq_rest[:, :]))
                if k < 2:
                    step(nc.vector.tensor_tensor(sq_rest[:, :], sq_rest[:, :], sq_parts[:, :, k], ALU.subtract))
            dve.sem_inc(sq_ready, 1)

            def search(i, par):
                def body():
                    dve.wait_ge(near_copied, i * NCH + NCH)
                    dve.nop(nofuse=True)
                    step(nc.vector.max(top8[par][:, :], near[par]))
                    dve.nop(nofuse=True)
                    nc.vector.max_index(idx8[par][:, :], top8[par][:, :], near[par]).then_inc(near_used, 1)
                    dve.wait_ge(near_used, i + 1)
                    nc.vector.tensor_copy(S[:, bass.ds(i, 1), :].rearrange("p i k -> p (i k)"), top8[par][:, 0:TOP])
                    step(nc.vector.tensor_copy(idx[:, bass.ds(i, 1), :].rearrange("p i k -> p (i k)"),
                                               idx8[par][:, 0:TOP]))
                counted("search", i, body)
            search(0, 0)
            search(1, 1)
            with dve.Fori(1, KT // 2) as pair:
                search(pair * 2, 0)
                search(pair * 2 + 1, 1)
            close("search", KT)

            step(nc.vector.scalar_tensor_tensor(S[:, :, :], S[:, :, :], -2.0 / (Z_SCALE * Z_SCALE),
                                                sq[:, :].unsqueeze(2).to_broadcast([P, KT, TOP]), ALU.mult, ALU.add))
            step(nc.vector.tensor_scalar(S[:, :, :], S[:, :, :], 0.0, None, ALU.max))
            dve.sem_inc(d2_ready, 1)
            dve.wait_ge(S_ready, 2)
            step(nc.vector.tensor_reduce(droot[:, :], S[:, :, :], AXX, ALU.add))
            step(nc.vector.tensor_tensor(droot[:, :], droot[:, :], rs[:, :], ALU.add))
            dve.sem_inc(deg_ready, 1)
            dve.wait_ge(root_ready, 2)
            step(nc.vector.reciprocal(dinv2[:, :], droot[:, :]))

            def make_y(c, par, m):
                def body():
                    dve.wait_ge(xin_loaded, 16 * nth(XIN, "y", c))
                    dve.wait_ge(xout_stored, 16 * (nth(XOUT, "y", c) - 1))
                    dve.wait_ge(yop_ready, nth(YOP, "y", c) - 1)
                    nc.vector.tensor_tensor(xout[:, :, :], xin[:, :, :], per_row(dinv2, c), ALU.mult
                                            ).then_inc(xout_ready, 1)
                    dve.wait_ge(xout_ready, nth(XOUT, "y", c))
                    dve.sem_inc(xin_free, 1)
                    split("y", xout[:, :, :], c)
                counted("y", c, body)
            each_chunk(dve, make_y)
            close("y")

            epilogues(4)
            epilogues(5)

        def first(c):
            return isinstance(c, int) and c == 0

        def pe_turn(pe, p, c):
            if p == 3:
                pe.wait_ge(z_ready, c + 1)
                src = xout
            elif p == 4:
                pe.wait_ge(mix_ready, c + 1)
                src = t_nat
            else:
                pe.wait_ge(xin_loaded, 16 * nth(XIN, p, c))
                src = xin
            if not first(c):
                if p == 3:
                    pe.wait_ge(zT_read, c)
                else:
                    pe.wait_ge(xT_ready, nth(XTS, p, c) - 1)
            elif p == 3:
                pe.wait_ge(xT_ready, nth(XTS, 2, NCH - 1))
            elif p == 4:
                pe.wait_ge(zT_read, NCH)
            elif p == 5:
                pe.wait_ge(xT_ready, nth(XTS, 4, NCH - 1))
            for t in range(TPC):
                last = nc.tensor.transpose(pxT[:, t * P:(t + 1) * P], src[:, t, :], ident[:, :])
            last.then_inc(xT_full, 1)

        def pe_project(pe, p, c):
            n = nth(ALL, p, c)
            pe.wait_ge(hT_ready, n)
            if p == 5:
                pe.wait_ge(xT_ready, nth(XTS, 5, c))
            if not (p == 0 and first(c)):
                pe.wait_ge(nat_read, n - 1)
            for t in range(TPC):
                h = hT[:, t * P:(t + 1) * P]
                if p == 1:
                    last = nc.tensor.transpose(pnat[:, t, :], h, ident[:, :])
                elif p == 5:
                    nc.tensor.matmul(pnat[:, t, :], xT[:, t * P:(t + 1) * P], wT[:, 1, :], start=True, stop=False)
                    last = nc.tensor.matmul(pnat[:, t, :], h, wT[:, 2, :], start=False, stop=True)
                else:
                    w = {0: w0_sb[:, :], 2: wT[:, 0, :], 3: wz_sb[:, :], 4: w2_sb[:, :]}[p]
                    last = nc.tensor.matmul(pnat[:, t, :], h, w, start=True, stop=True)
            last.then_inc(nat_full, 1)

        TURN_AT = {2: 2, 3: 20, 4: 12, 5: 2}
        PROJECT_AT = {0: 8, 1: 4, 2: 10, 3: 3, 4: 20, 5: 10}

        def pe_epilogue_at(pe, kt, p, c):
            if TURN_AT.get(p) == kt:
                pe_turn(pe, p, c)
            if PROJECT_AT[p] == kt:
                pe_project(pe, p, c)

        def pe_epilogue(pe, p, c):
            for kt in range(KT):
                pe_epilogue_at(pe, kt, p, c)

        def products(p, par, kt, high, low):
            y = yop[OPERAND[p]]
            nc.tensor.matmul(acc[par][:, :], y[:, 0, kt, :], high, start=(kt == 0), stop=False)
            nc.tensor.matmul(acc[par][:, :], y[:, 0, kt, :], low, start=False, stop=False)
            return nc.tensor.matmul(acc[par][:, :], y[:, 1, kt, :], high, start=False, stop=(kt == KT - 1))

        @block.tensor
        def _(pe):
            pe.wait_ge(ident_made, 3)
            pe.wait_ge(par_loaded, 16 * PARAMS)
            for k in range(3):
                last = nc.tensor.transpose(pt[0][:, k * D:(k + 1) * D], t_nat[:, k, :], ident[:, :])
            last.then_inc(setup_pe, 1)
            pe.wait_ge(setup_dve, 1)
            rows_j = JD * KT
            nc.tensor.transpose(pt[1][:, 0:rows_j], hT[0:rows_j, 0:P], ident[0:rows_j, 0:rows_j]).then_inc(setup_pe, 1)
            pe.wait_ge(setup_dve, SETUP_DVE)
            pe.wait_ge(y0_ready, 1)

            def transposing_chunk(c, par, m):
                def products_of(kt):
                    pe.wait_ge(low_done, c * KT + kt + 1)
                    if kt < KEPT:
                        hi, lo = (kept[:, bass.ds(c, 1), kt, h, :].rearrange("p c n -> p (c n)") for h in range(2))
                    else:
                        s = (par * UPC + (kt - KEPT) // UNIT) % 2
                        hi, lo = (stage[s][:, (kt - KEPT) % UNIT, h, :] for h in range(2))
                    if kt == 0 and not (isinstance(c, int) and c < 2):
                        pe.wait_ge(hT_ready, c - 1)
                    last = products(0, par, kt, hi, lo)
                    if kt == KT - 1:
                        last.then_inc(acc_full, 1)
                    if kt >= KEPT and (kt - KEPT) % UNIT == UNIT - 1:
                        pe.wait_ge(acc_full, c + 1) if kt == KT - 1 else None
                        if kt == KT - 1:
                            pe.sem_inc(stage_used, 1)
                        else:
                            last.then_inc(stage_used, 1)

                for kt in range(KT):
                    u = kt // TPC
                    if kt % TPC == 0:
                        pe.wait_ge(nat_loaded[u % 4], 16 * (c * 2 + u // 4 + 1))
                    if not (first(c) and kt < 4):
                        pe.wait_ge(low_done, c * KT + kt - 3)
                    for t in range(TPC):
                        last = nc.tensor.transpose(pt[kt % 4][:, t * P:(t + 1) * P],
                                                   nat[u % 4][:, t, (kt % TPC) * P:(kt % TPC + 1) * P], ident[:, :])
                    last.then_inc(tr_done, 1)
                    if not first(c):
                        pe_epilogue_at(pe, kt, 0, c - 1)
                    if kt >= LAG:
                        products_of(kt - LAG)
                for kt in range(KT - LAG, KT):
                    products_of(kt)
            each_chunk(pe, transposing_chunk)

            def product_pass(p, before):
                source = "y" if p == 4 else p - 1
                def chunk(c, par, m):
                    n = nth(ALL, p, c)
                    pe.wait_ge(hT_ready, n - 2)
                    for kt in range(KT):
                        if first(c) and kt % TPC == 0:
                            pe.wait_ge(yop_ready, nth(YOP, source, kt // TPC))
                        if kt < KEPT:
                            hi, lo = (kept[:, bass.ds(c, 1), kt, h, :].rearrange("p c n -> p (c n)") for h in range(2))
                        else:
                            u = (kt - KEPT) // UNIT
                            if (kt - KEPT) % UNIT == 0:
                                pe.wait_ge(unit_loaded[u], 16 * ((p - 1) * NCH + c + 1))
                            hi, lo = (ring[u][:, (kt - KEPT) % UNIT, h, :] for h in range(2))
                        last = products(p, par, kt, hi, lo)
                        if kt == KT - 1:
                            last.then_inc(acc_full, 1)
                            pe.wait_ge(acc_full, n)
                            pe.sem_inc(unit_used, 1)
                        elif kt >= KEPT and (kt - KEPT) % UNIT == UNIT - 1:
                            last.then_inc(unit_used, 1)
                        if not first(c):
                            pe_epilogue_at(pe, kt, p, c - 1)
                        elif before is not None:
                            pe_epilogue_at(pe, kt, before, NCH - 1)
                each_chunk(pe, chunk)

            product_pass(1, 0)
            product_pass(2, 1)
            product_pass(3, 2)
            pe_epilogue(pe, 3, NCH - 1)

            pe.wait_ge(sq_ready, 1)
            pe.wait_ge(hT_ready, nth(ALL, 3, NCH - 1))
            for c in range(NCH):
                if c >= 2:
                    pe.wait_ge(sqT_ready, c - 1)
                for t in range(TPC):
                    last = nc.tensor.transpose(sq_bank(c)[:, t * P:(t + 1) * P], sq_parts[:, c * TPC + t, :], ident16[:, :])
                last.then_inc(sqT_full, 1)
            pe.wait_ge(sqT_ready, NCH)
            pe.wait_ge(zT_read, NCH)

            def closeness(i):
                zh, zl = (zT[:, h, bass.ds(i * P, P)] for h in range(2))
                for j in range(NCH):
                    cols = slice(j * CHUNK, (j + 1) * CHUNK)
                    if not (first(i) and j < 4):
                        pe.wait_ge(near_copied, i * NCH + j - 3)
                    nc.tensor.matmul(pt[j % 4][:, :], zh, zT[:, 0, cols], start=True, stop=False)
                    nc.tensor.matmul(pt[j % 4][:, :], zh, zT[:, 1, cols], start=False, stop=False)
                    nc.tensor.matmul(pt[j % 4][:, :], zl, zT[:, 0, cols], start=False, stop=False)
                    nc.tensor.matmul(pt[j % 4][:, :], ones3[:, :], sqT[:, cols], start=False, stop=True
                                     ).then_inc(near_full, 1)
            closeness(0)
            with pe.Fori(1, KT) as i:
                closeness(i)

            product_pass(4, None)
            product_pass(5, 4)
            pe_epilogue(pe, 5, NCH - 1)


PARAMS = 13
SETUP_DVE = 6

_INS = ["x", "adj", "L0_gnn_d_list", "L0_gnn_weight", "L0_gnn_filt", "L0_gnn_bias", "L1_gnn_alpha", "L1_gnn_W",
        "L1_gnn_b", "L2_gnn_W1", "L2_gnn_b1", "L2_gnn_W2", "L2_gnn_b2", "L3_gnn_W", "L3_gnn_b"]


def kernel(**inputs):
    import numpy as np
    import concourse.bacc as bacc
    from concourse.bass_utils import run_bass_kernel_spmd

    nc = bacc.Bacc("TRN2", target_bir_lowering=False, num_devices=1, dynamic_dma_scratch_size=4096)
    arrays, args = {}, []
    for name in _INS:
        a = np.ascontiguousarray(inputs[name])
        arrays[f"in_{name}"] = a
        args.append(nc.dram_tensor(f"in_{name}", a.shape, mybir.dt.from_np(a.dtype), kind="ExternalInput").ap())
    out = nc.dram_tensor("out_x", inputs["x"].shape, F32, kind="ExternalOutput").ap()
    gnn_kernel(nc, *args, out)
    r = run_bass_kernel_spmd(nc, [arrays], core_ids=[0])
    return r.results[0]["out_x"]
```

```python
from contextlib import ExitStack

import concourse.bass as bass
from concourse import mybir

F32 = mybir.dt.float32
F16 = mybir.dt.float16
BF16 = mybir.dt.bfloat16
U32 = mybir.dt.uint32
ALU = mybir.AluOpType
ACT = mybir.ActivationFunctionType
AXX = mybir.AxisListType.X

P = 128
CHUNK = 512
TPC = CHUNK // P
KEPT = 7
UNIT = 5
STORES = [(0, 3), (3, 5)]
LAG = 3
TOP = 4
LAST = 5

A_SCALE = 16.0
Z_SCALE = 4.0
Y_SCALE = {-1: 32.0, 0: 4.0, 1: 128.0, 2: 64.0, 3: 64.0, 4: 128.0}
OPERAND = [0, 1, 0, 1, 1, 0]


def gnn_kernel(nc, x, adj, d_list, w0, filt, bias0, alpha, w1, b1, wz, bz, w2, b2, w3, b3, out):
    N, D = x.shape
    JD = d_list.shape[0]
    KT = N // P
    NCH = N // CHUNK
    NAT_UNITS = KT // TPC
    UPC = (KT - KEPT) // UNIT
    assert D == P and UPC * UNIT + KEPT == KT and NCH % 2 == 0

    at_dram = nc.dram_tensor("at_scratch", [NCH, UPC, P, UNIT * 2 * CHUNK], F16).ap()
    x_dram = [None, nc.dram_tensor("x1_scratch", [N, D], F32).ap(), nc.dram_tensor("x2_scratch", [N, D], F32).ap(),
              nc.dram_tensor("x3_scratch", [N, D], F32).ap()]
    x_dram[0] = x
    y_dram = nc.dram_tensor("y_scratch", [N, D], F32).ap()

    with ExitStack() as ctx:
        def sb(name, shape, dt):
            return ctx.enter_context(nc.sbuf_tensor(name, shape, dt))

        def ps(name, shape, dt=F32):
            return ctx.enter_context(nc.psum_tensor(name, shape, dt))

        def sem(name):
            return ctx.enter_context(nc.semaphore(name))

        kept = sb("kept", [P, NCH, KEPT, 2, CHUNK], F16)
        slot_elems = UNIT * 2 * CHUNK
        nat_elems = TPC * CHUNK * 2
        region = sb("region", [P, 4 * nat_elems + 2 * slot_elems], F16)
        ring = [region[:, s * slot_elems:(s + 1) * slot_elems].rearrange("p (k h n) -> p k h n", k=UNIT, h=2)
                for s in range(UPC)]
        nat = [region[:, s * nat_elems:(s + 1) * nat_elems].bitcast(F32).rearrange("p (t k) -> p t k", t=TPC)
               for s in range(4)]
        stage_flat = [region[:, 4 * nat_elems + s * slot_elems:4 * nat_elems + (s + 1) * slot_elems] for s in range(2)]
        stage = [s.rearrange("p (k h n) -> p k h n", k=UNIT, h=2) for s in stage_flat]
        x0 = region[:, 4 * nat_elems:4 * nat_elems + 2 * KT * D].bitcast(F32).rearrange("p (t f) -> p t f", t=KT)
        region_elems = 4 * nat_elems + 2 * slot_elems
        near = [region[:, region_elems - (s + 1) * 2 * N:region_elems - s * 2 * N].bitcast(F32) for s in range(2)]
        y_all = near[0].rearrange("p (t f) -> p t f", t=KT)
        Y_SLOT = (region_elems - 2 * N) // slot_elems
        sqT = region[:, 0:N].bitcast(BF16)

        yop = [sb(f"yop{b}", [P, 2, KT, D], F16) for b in range(2)]
        zT = yop[0][:, :, :, :].rearrange("p h t f -> p h (t f)")
        hT = sb("hT", [P, CHUNK], F32)
        mixed = sb("mixed", [P, TPC, D], F32)
        xT = sb("xT", [P, CHUNK], F32)
        t_nat = sb("t_nat", [P, TPC, D], F32)
        xin = sb("xin", [P, TPC, D], F32)
        xout = sb("xout", [P, TPC, D], F32)
        gath = [sb(f"gath{b}", [P, TPC, D], F32) for b in range(2)]
        ident = sb("ident", [P, P], F32)
        w0_sb, wz_sb = (sb(n, [D, D], F32) for n in ("w0_sb", "wz_sb"))
        w2_sb = w0_sb
        wT = sb("wT", [D, 3, D], F32)
        ident16 = wT[:, 0, 0:D // 2].bitcast(BF16)
        bias = {k: sb(f"bias{k}", [P, D], F32) for k in (1, 2, 3)}
        bias[4], bias[5] = bias[2], bias[1]
        alpha_c = sb("alpha_c", [P, 1], F32)
        alpha_acc = sb("alpha_acc", [P, 1], F32)
        one_alpha = sb("one_alpha", [P, 1], F32)
        eps_ln = sb("eps_ln", [P, 1], F32)
        eps_d2 = sb("eps_d2", [P, 1], F32)
        scale = sb("scale", [P, KT], F32)
        rs_part = [sb(f"rs_part{b}", [P, NAT_UNITS, TPC], F32) for b in range(2)]
        rs = sb("rs", [P, KT], F32)
        inv_deg = sb("inv_deg", [P, KT], F32)
        zero_deg = sb("zero_deg", [P, KT], F32)
        dinv = sb("dinv", [P, KT], F32)
        dinv2 = inv_deg
        droot = sb("droot", [P, KT], F32)
        stats = sb("stats", [P, TPC, 6], F32)
        mv = sb("mv", [P, TPC, 2], F32)
        std = sb("std", [P, TPC], F32)
        rstd = sb("rstd", [P, TPC], F32)
        sq = sb("sq", [P, KT], F32)
        sq_rest = zero_deg
        sq_parts = sb("sq_parts", [P, KT, 3], BF16)
        ones3 = sb("ones3", [P, P], BF16)
        top8 = [sb(f"top8_{b}", [P, 8], F32) for b in range(2)]
        idx8 = [sb(f"idx8_{b}", [P, 8], U32) for b in range(2)]
        S = sb("S", [P, KT, TOP], F32)
        idx = sb("idx", [P, KT, TOP], U32)
        idx_chunk = [sb(f"idx_chunk{b}", [P, TPC, TOP], U32) for b in range(2)]

        acc = [ps(f"acc{b}", [P, CHUNK]) for b in range(2)]
        pt = [ps(f"pt{b}", [P, CHUNK]) for b in range(4)]
        pnat = ps("pnat", [P, TPC, D])
        pxT = ps("pxT", [P, CHUNK])


        def sq_bank(c):
            return acc[c % 2][:, :].bitcast(BF16)[0:3, 0:CHUNK]

        x0_loaded, late_loaded, consts, ident_made = sem("x0_loaded"), sem("late_loaded"), sem("consts"), sem("ident_made")
        par_loaded = [sem(f"par_loaded{q}") for q in range(2)]
        y0_ready = sem("y0_ready")
        setup_pe, setup_dve = sem("setup_pe"), sem("setup_dve")
        nat_loaded = [sem(f"nat_loaded{s}") for s in range(4)]
        rows_summed_act, rows_summed_dve = sem("rows_summed_act"), sem("rows_summed_dve")
        tr_done, high_done, low_done = sem("tr_done"), sem("high_done"), sem("low_done")
        stage_used = sem("stage_used")
        stage_stored = [[sem(f"stage_stored{s}_{part}") for part in range(len(STORES))] for s in range(2)]
        unit_loaded = [sem(f"unit_loaded{s}") for s in range(UPC)]
        unit_used = sem("unit_used")
        acc_full, hT_ready, nat_full, nat_read = sem("acc_full"), sem("hT_ready"), sem("nat_full"), sem("nat_read")
        xT_full, xT_ready, zT_read = sem("xT_full"), sem("xT_ready"), sem("zT_read")
        xin_loaded, xin_free = sem("xin_loaded"), sem("xin_free")
        var_ready, std_ready, yop_ready = sem("var_ready"), sem("std_ready"), sem("yop_ready")
        xout_ready, xout_stored = sem("xout_ready"), sem("xout_stored")
        z_ready = sem("z_ready")
        chain_dve, rows_closed = sem("chain_dve"), sem("rows_closed")
        sq_ready, sqT_full, sqT_ready = sem("sq_ready"), sem("sqT_full"), sem("sqT_ready")
        near_full, near_copied, near_used = sem("near_full"), sem("near_copied"), sem("near_used")
        d2_ready, S_ready, deg_ready, root_ready = sem("d2_ready"), sem("S_ready"), sem("deg_ready"), sem("root_ready")
        idx_ready, gath_used = sem("idx_ready"), sem("gath_used")
        gath_loaded = [sem(f"gath_loaded{b}") for b in range(2)]
        mix_ready = sem("mix_ready")
        x2_loaded, y_scaled, y_stored = sem("x2_loaded"), sem("y_scaled"), sem("y_stored")

        def nth(passes, p, c):
            return passes.index(p) * NCH + c + 1

        ALL = [0, 1, 2, 3, 4, 5]
        XT = [2, 3, 4, 5]
        XTS = [2, 4, 5]
        XIN = [1, 2, 4, 5]
        YOP = [0, 1, 2, "y", 4]

        def each_chunk(eng, body, peel_last=False):
            body(0, 0, 0)
            body(1, 1, 0)
            with eng.Fori(1, NCH // 2 - peel_last) as pair:
                body(pair * 2, 0, pair)
                body(pair * 2 + 1, 1, pair)
            if peel_last:
                body(NCH - 2, 0, NCH // 2 - 1)
                body(NCH - 1, 1, NCH // 2 - 1)

        def first(c):
            return isinstance(c, int) and c == 0

        def among_first(c, n):
            return isinstance(c, int) and c < n

        def rows(t, c):
            return t[bass.ds(c * CHUNK, CHUNK), :].rearrange("(t p) f -> p t f", p=P)

        def per_row(v, c):
            return v[:, bass.ds(c * TPC, TPC)].unsqueeze(2).to_broadcast([P, TPC, D])

        def over_tiles(v):
            return v[:, :].unsqueeze(1).to_broadcast([P, TPC, D])

        PARAM_LOADS = [(t_nat[:, 0, :], w1), (t_nat[:, 1:3, :], w3.rearrange("o (h f) -> o h f", h=2)),
                       (hT[0:JD * KT, 0:P], d_list.rearrange("j (t p) -> (j t) p", p=P)),
                       (hT[0:JD * KT, P:2 * P], filt.rearrange("j (t p) -> (j t) p", p=P)),
                       (w0_sb[:, :], w0), (wz_sb[:, :], wz), (bias[1][:, :], bias0.partition_broadcast(P)),
                       (bias[2][:, :], b1.partition_broadcast(P)), (bias[3][:, :], bz.partition_broadcast(P)),
                       (alpha_c[:, :], alpha.partition_broadcast(P))]
        PARAMS = len(PARAM_LOADS)

        block = ctx.enter_context(nc.Block())

        @block.sync
        def _(sp):
            for loaded in par_loaded:
                sp.wait_ge(loaded, 16 * PARAMS // 2)

            def load_natural(c, par, m):
                for u in range(NAT_UNITS):
                    s = u % 4
                    if not (first(c) and u < 4):
                        before = c * NAT_UNITS + (u - 4) + 1
                        sp.wait_ge(tr_done, before * TPC)
                        sp.nop(nofuse=True)
                        half = c * (NAT_UNITS // 2) + (u - 4) // 2 + 1
                        sp.wait_ge(rows_summed_dve if u % 2 == 0 else rows_summed_act, half)
                    sp.dma_start(nat[s], adj[bass.ds(c * CHUNK, CHUNK), u * CHUNK:(u + 1) * CHUNK]
                                 .rearrange("(t p) k -> p t k", p=P)).then_inc(nat_loaded[s], 16)
                    if first(c) and u == 0:
                        sp.dma_start(x0, x.rearrange("(t p) f -> p t f", p=P)).then_inc(x0_loaded, 16)
            each_chunk(sp, load_natural)

            sp.wait_ge(tr_done, NCH * KT)
            sp.wait_ge(rows_summed_dve, NCH * NAT_UNITS // 2)
            sp.wait_ge(rows_summed_act, NCH * NAT_UNITS // 2)
            sp.wait_ge(stage_used, NCH * UPC)
            for s in range(2):
                for part in range(len(STORES)):
                    sp.wait_ge(stage_stored[s][part], 16 * NCH * UPC // 2)

            def stream(p):
                def units(c, par, m):
                    for u in range(UPC):
                        if p == 4 and first(c) and u == Y_SLOT:
                            sp.wait_ge(y_stored, 16)
                            sp.wait_ge(yop_ready, nth(YOP, "y", NCH - 1))
                        if p > 1 or not first(c):
                            sp.wait_ge(unit_used, (p - 1) * NCH * UPC + c * UPC + u - UPC + 1)
                        sp.dma_start(ring[u].rearrange("p k h n -> p (k h n)"),
                                     at_dram[bass.ds(c, 1), u, :, :].rearrange("c p n -> (c p) n")
                                     ).then_inc(unit_loaded[u], 16)
                each_chunk(sp, units)

            stream(1)
            stream(2)
            stream(3)
            sp.wait_ge(xout_stored, 16 * nth(XIN, 2, NCH - 1))
            sp.wait_ge(near_used, KT - 1)
            sp.dma_start(y_all, x_dram[2].rearrange("(t p) f -> p t f", p=P)).then_inc(x2_loaded, 16)
            sp.wait_ge(near_used, KT)
            stream(4)
            stream(5)

        @block.gpsimd
        def _(pool):
            pool.memset(ident[:, :], 0.0).then_inc(ident_made, 1)
            pool.memset(ones3[:, :], 0.0).then_inc(ident_made, 1)
            pool.memset(eps_ln[:, :], 1e-5).then_inc(consts, 1)
            pool.memset(eps_d2[:, :], 1e-10).then_inc(consts, 1)
            pool.wait_ge(ident_made, 2)
            pool.memset(ones3[0:3, :], 1.0).then_inc(consts, 1)
            pool.affine_select(out=ident[:, :], in_=ident[:, :], compare_op=ALU.not_equal, fill=1.0, base=0,
                               pattern=[[-1, P]], channel_multiplier=1).then_inc(ident_made, 1)

            for dst, src in PARAM_LOADS[1::2]:
                pool.dma_start(dst, src).then_inc(par_loaded[1], 16)

            def store_units(c, par, m):
                for u in range(UPC):
                    s = (par * UPC + u) % 2
                    for part, (k0, k1) in enumerate(STORES):
                        pool.wait_ge(low_done, c * KT + KEPT + u * UNIT + k1)
                        pool.nop(nofuse=True)
                        cols = slice(k0 * 2 * CHUNK, k1 * 2 * CHUNK)
                        pool.dma_start(at_dram[bass.ds(c, 1), u, :, cols].rearrange("c p n -> (c p) n"),
                                       stage_flat[s][:, cols]).then_inc(stage_stored[s][part], 16)
            each_chunk(pool, store_units)

            def load_xin(p, source, c, fresh=False):
                if not fresh:
                    pool.wait_ge(xin_free, nth(XIN, p, c) - 1)
                pool.nop(nofuse=True)
                pool.dma_start(xin[:, :, :], rows(source, c)).then_inc(xin_loaded, 16)

            def residual_pass(p, source):
                if p > 1:
                    pool.wait_ge(xout_stored, 16 * nth(XIN, p, -1))
                each_chunk(pool, lambda c, par, m: load_xin(p, source, c, p == 1 and first(c)))

            residual_pass(1, x_dram[0])
            residual_pass(2, x_dram[1])

            pool.wait_ge(xout_stored, 16 * nth(XIN, 2, NCH - 1))
            for dst, src in [(w2_sb[:, :], w2), (bias[4][:, :], b2.partition_broadcast(P)),
                             (bias[5][:, :], b3.partition_broadcast(P))]:
                pool.dma_start(dst, src).then_inc(late_loaded, 16)

            def gather_pass(c, par, m):
                pool.wait_ge(idx_ready, c + 1)
                for t in range(TPC):
                    if not (first(c) and t < 2):
                        pool.wait_ge(gath_used, c * TPC + t - 1)
                    pool.nop(nofuse=True)
                    for r in range(TOP):
                        pool.indirect_dma_start(gath[t % 2][:, r, :], None, y_dram,
                                                bass.IndirectOffsetOnAxis(ap=idx_chunk[par][:, t, r:r + 1], axis=0)
                                                ).then_inc(gath_loaded[t % 2], 16)
                load_xin(4, x_dram[2], c)
            pool.wait_ge(y_stored, 16)
            each_chunk(pool, gather_pass)

            residual_pass(5, x_dram[3])

        def act_epilogue(act, p, c, par):
            n = nth(ALL, p, c)
            if p in (2, 4, 5):
                act.wait_ge(xT_full, nth(XT, p, c))
                if not (p == 2 and first(c)):
                    act.wait_ge(nat_full, n - 1)
                    act.wait_ge(hT_ready, n - 1)
                nc.scalar.activation(xT[:, :], pxT[:, :], ACT.Copy,
                                     scale=one_alpha[:, 0:1] if p == 2 else 1.0).then_inc(xT_ready, 1)
            if p in (0, 1, 3, 5):
                act.wait_ge(acc_full, n)
                if not (p == 0 and first(c)):
                    act.wait_ge(nat_full, n - 1)
                nc.scalar.activation(hT[:, :], acc[par][:, :], ACT.Copy,
                                     scale=1.0 / (A_SCALE * Y_SCALE[p - 1])).then_inc(hT_ready, 1)
            if p in XIN:
                act.wait_ge(var_ready, nth(XIN, p, c))
                nc.scalar.activation(std[:, :], mv[:, :, 1], ACT.Sqrt, bias=eps_ln[:, 0:1]).then_inc(std_ready, 1)
                target = {1: x_dram[1], 2: x_dram[2], 4: x_dram[3], 5: out}[p]
                act.wait_ge(xout_ready, nth(XIN, p, c))
                act.nop(nofuse=True)
                act.dma_start(rows(target, c), xout[:, :, :]).then_inc(xout_stored, 16)

        @block.scalar
        def _(act):
            for dst, src in PARAM_LOADS[::2]:
                act.dma_start(dst, src).then_inc(par_loaded[0], 16)
            act.wait_ge(consts, 3)
            act.wait_ge(setup_dve, SETUP_DVE)

            def split_high(c, par, m):
                for kt in range(KT):
                    g = c * KT + kt
                    act.wait_ge(tr_done, g + 1)
                    if kt < KEPT:
                        dst = kept[:, bass.ds(c, 1), kt, 0, :].rearrange("p c n -> p (c n)")
                    else:
                        u = (kt - KEPT) // UNIT
                        s = (par * UPC + u) % 2
                        if first(c) and kt == KEPT:
                            act.wait_ge(y0_ready, 1)
                        if (kt - KEPT) % UNIT == 0 and not (isinstance(c, int) and c * UPC + u < 2):
                            before = c * UPC + u - 1
                            act.wait_ge(stage_used, before)
                        for part, (k0, k1) in enumerate(STORES):
                            if (kt - KEPT) % UNIT == k0 and not (isinstance(c, int) and c * UPC + u < 2):
                                act.wait_ge(stage_stored[s][part], 16 * (m * UPC + (par * UPC + u) // 2))
                        dst = stage[s][:, (kt - KEPT) % UNIT, 0, :]
                    nc.scalar.activation(dst, pt[kt % 4][:, :], ACT.Copy, scale=A_SCALE).then_inc(high_done, 1)
                    if kt % 8 == 6:
                        u = kt // TPC
                        act.wait_ge(nat_loaded[u % 4], 16 * (c * 2 + u // 4 + 1))
                        if u == 1 and not among_first(c, 2):
                            act.wait_ge(rows_closed, c - 1)
                        if not (first(c) and u == 1):
                            act.wait_ge(rows_summed_act, c * (NAT_UNITS // 2) + u // 2)
                        for t in range(TPC):
                            discard = (xin, xout)[t // 2][:, :, :].rearrange("p t f -> p (t f)").bitcast(BF16)
                            last = nc.scalar.activation(discard[:, (t % 2) * CHUNK:(t % 2 + 1) * CHUNK],
                                                        nat[u % 4][:, t, :], ACT.Copy,
                                                        accum_out=rs_part[par][:, u, t:t + 1])
                        last.then_inc(rows_summed_act, 1)
                    if kt == 8 and not first(c):
                        act_epilogue(act, 0, c - 1, 1 - par)
            each_chunk(act, split_high)
            act_epilogue(act, 0, NCH - 1, 1)
            act.wait_ge(deg_ready, 1)
            nc.scalar.activation(droot[:, :], rs[:, :], ACT.Sqrt).then_inc(root_ready, 1)

            for p in (1, 2, 3):
                each_chunk(act, lambda c, par, m, p=p: act_epilogue(act, p, c, par))

            for c in range(NCH):
                act.wait_ge(sqT_full, c + 1)
                nc.scalar.activation(sqT[0:3, c * CHUNK:(c + 1) * CHUNK], sq_bank(c), ACT.Copy).then_inc(sqT_ready, 1)

            def copy_near(i, par):
                if not among_first(i, 2):
                    act.wait_ge(near_used, i - 1)
                for j in range(NCH):
                    act.wait_ge(near_full, i * NCH + j + 1)
                    nc.scalar.activation(near[par][:, j * CHUNK:(j + 1) * CHUNK], pt[j % 4][:, :],
                                         ACT.Copy).then_inc(near_copied, 1)
            copy_near(0, 0)
            copy_near(1, 1)
            with act.Fori(1, KT // 2) as pair:
                copy_near(pair * 2, 0)
                copy_near(pair * 2 + 1, 1)

            act.wait_ge(d2_ready, 1)
            nc.scalar.activation(S[:, :, :], S[:, :, :], ACT.Sqrt, bias=eps_d2[:, 0:1]).then_inc(S_ready, 1)
            act.wait_ge(S_ready, 1)
            nc.scalar.activation(S[:, :, :], S[:, :, :], ACT.Exp, scale=-0.5).then_inc(S_ready, 1)
            act.wait_ge(deg_ready, 2)
            nc.scalar.activation(droot[:, :], droot[:, :], ACT.Sqrt).then_inc(root_ready, 1)

            act.wait_ge(y_scaled, NCH)
            act.dma_start(y_dram.rearrange("(t p) f -> p t f", p=P), y_all).then_inc(y_stored, 16)

            for p in (4, 5):
                each_chunk(act, lambda c, par, m, p=p: act_epilogue(act, p, c, par))
            act.wait_ge(xout_stored, 16 * nth(XIN, 5, NCH - 1))

        @block.vector
        def _(dve):
            count = [0]

            def step(ins):
                count[0] = count[0] + 1
                ins.then_inc(chain_dve, 1)
                dve.wait_ge(chain_dve, count[0])

            steps_of = {}
            start_of = {}

            def counted(kind, c, body):
                if first(c):
                    start_of[kind] = count[0]
                else:
                    count[0] = c * steps_of[kind] + start_of[kind]
                before = count[0]
                body()
                if first(c):
                    steps_of[kind] = count[0] - before

            def close(kind, chunks=NCH):
                count[0] = start_of[kind] + chunks * steps_of[kind]

            def split(p, src, c):
                k = 3 if p == "y" else p
                buf = yop[OPERAND[k + 1]]
                hi, lo = buf[:, 0, bass.ds(c * TPC, TPC), :], buf[:, 1, bass.ds(c * TPC, TPC), :]
                step(nc.vector.tensor_scalar(hi, src, Y_SCALE[k], None, ALU.mult))
                nc.vector.scalar_tensor_tensor(lo, src, Y_SCALE[k], hi, ALU.mult, ALU.subtract).then_inc(yop_ready, 1)

            def layernorm(p, c):
                for t in range(TPC):
                    last = nc.vector.bn_stats(stats[:, t, :], t_nat[:, t, :])
                step(last)
                dve.nop(nofuse=True)
                for t in range(TPC):
                    last = nc.vector.bn_aggr(mv[:, t, :], stats[:, t, :])
                last.then_inc(var_ready, 1)
                dve.wait_ge(std_ready, nth(XIN, p, c))
                step(nc.vector.reciprocal(rstd[:, :], std[:, :]))
                if not (p == 1 and first(c)):
                    dve.wait_ge(xout_stored, 16 * (nth(XIN, p, c) - 1))
                for t in range(TPC):
                    last = nc.vector.tensor_scalar(xout[:, t, :], t_nat[:, t, :], mv[:, t, 0:1], rstd[:, t:t + 1],
                                                   ALU.subtract, ALU.mult)
                last.then_inc(xout_ready, 1)
                dve.wait_ge(xout_ready, nth(XIN, p, c))

            def give_indices(c, par):
                nc.vector.tensor_copy(idx_chunk[par][:, :, :], idx[:, bass.ds(c * TPC, TPC), :]).then_inc(idx_ready, 1)

            def mix(c, tiles):
                for t in tiles:
                    dve.wait_ge(gath_loaded[t % 2], 16 * TOP * (c * 2 + t // 2 + 1))
                    g = gath[t % 2]
                    weight = S[:, bass.ds(c * TPC + t, 1), :].rearrange("p t r -> p (t r)")
                    step(nc.vector.tensor_tensor(g[:, :, :], g[:, :, :], weight.unsqueeze(2).to_broadcast([P, TOP, D]),
                                                 ALU.mult))
                    nc.vector.tensor_reduce(mixed[:, t, :], g[:, :, :].rearrange("p r f -> p f r"), AXX, ALU.add
                                            ).then_inc(gath_used, 1)
                if tiles[-1] == TPC - 1:
                    dve.wait_ge(gath_used, c * TPC + TPC)
                    dve.sem_inc(mix_ready, 1)

            def epilogue(p, c, par):
                n = nth(ALL, p, c)
                last_chunk = isinstance(c, int) and c == NCH - 1
                if p == 4 and not (isinstance(c, int) and c >= NCH - 2):
                    give_indices(c + 2, par)
                if p in (2, 4):
                    dve.wait_ge(xT_ready, nth(XTS, p, c))
                    dve.wait_ge(acc_full, n)
                    dve.wait_ge(nat_full, n - 1)
                    factor = alpha_acc[:, 0:1] if p == 2 else 1.0 / (A_SCALE * Y_SCALE[3])
                    nc.vector.scalar_tensor_tensor(hT[:, :], acc[par][:, :], factor, xT[:, :], ALU.mult,
                                                   ALU.add).then_inc(hT_ready, 1)
                if p == 4 and not last_chunk:
                    mix(c + 1, (0, 1))
                dve.wait_ge(nat_full, n)
                if p == 0:
                    nc.vector.tensor_tensor(t_nat[:, :, :], pnat[:, :, :], per_row(scale, c), ALU.mult).then_inc(nat_read, 1)
                    dve.wait_ge(nat_read, n)
                    split(0, t_nat[:, :, :], c)
                    return
                if p == 1:
                    dve.wait_ge(xin_loaded, 16 * nth(XIN, p, c))
                    nc.vector.tensor_tensor(t_nat[:, :, :], pnat[:, :, :], xin[:, :, :], ALU.add).then_inc(nat_read, 1)
                    dve.wait_ge(nat_read, n)
                    dve.sem_inc(xin_free, 1)
                    step(nc.vector.tensor_tensor(t_nat[:, :, :], t_nat[:, :, :], over_tiles(bias[1]), ALU.add))
                if p in (2, 3, 4):
                    factor = {2: inv_deg, 3: dinv, 4: dinv2}[p]
                    nc.vector.tensor_tensor(t_nat[:, :, :], pnat[:, :, :], per_row(factor, c), ALU.mult).then_inc(nat_read, 1)
                    dve.wait_ge(nat_read, n)
                    step(nc.vector.tensor_tensor(t_nat[:, :, :], t_nat[:, :, :], over_tiles(bias[p]), ALU.add))
                if p == 5:
                    nc.vector.tensor_tensor(t_nat[:, :, :], pnat[:, :, :], over_tiles(bias[5]), ALU.add).then_inc(nat_read, 1)
                    dve.wait_ge(nat_read, n)
                if p in (2, 4, 5):
                    dve.wait_ge(xin_loaded, 16 * nth(XIN, p, c))
                    if p == 4:
                        step(nc.vector.tensor_tensor(t_nat[:, :, :], t_nat[:, :, :], xin[:, :, :], ALU.add))
                    else:
                        step(nc.vector.scalar_tensor_tensor(t_nat[:, :, :], t_nat[:, :, :], 0.0, xin[:, :, :],
                                                            ALU.max, ALU.add))
                    dve.sem_inc(xin_free, 1)
                if p == 3:
                    if first(c):
                        dve.wait_ge(xout_stored, 16 * nth(XIN, 2, NCH - 1))
                    else:
                        dve.wait_ge(xT_full, nth(XT, 3, c) - 1)
                    step(nc.vector.scalar_tensor_tensor(xout[:, :, :], t_nat[:, :, :], 0.1, t_nat[:, :, :],
                                                        ALU.mult, ALU.max))
                    dve.sem_inc(z_ready, 1)
                    step(nc.vector.tensor_tensor(xin[:, :, :], xout[:, :, :], xout[:, :, :], ALU.mult))
                    step(nc.vector.tensor_reduce(sq[:, bass.ds(c * TPC, TPC)], xin[:, :, :], AXX, ALU.add))
                    dve.wait_ge(xT_full, nth(XT, 3, c))
                    zh = zT[:, 0, bass.ds(c * CHUNK, CHUNK)]
                    step(nc.vector.tensor_scalar(zh, pxT[:, :], Z_SCALE, None, ALU.mult))
                    nc.vector.scalar_tensor_tensor(zT[:, 1, bass.ds(c * CHUNK, CHUNK)], pxT[:, :], Z_SCALE, zh,
                                                   ALU.mult, ALU.subtract).then_inc(zT_read, 1)
                    return
                layernorm(p, c)
                if p == 2:
                    step(nc.vector.tensor_tensor(t_nat[:, :, :], xout[:, :, :], per_row(dinv, c), ALU.mult))
                    split(2, t_nat[:, :, :], c)
                elif p != LAST:
                    split(p, xout[:, :, :], c)
                if p == 4 and not last_chunk:
                    mix(c + 1, (2, 3))

            for loaded in par_loaded:
                dve.wait_ge(loaded, 16 * PARAMS // 2)
            rows_j = JD * KT
            step(nc.vector.tensor_tensor(hT[0:rows_j, P:2 * P], hT[0:rows_j, 0:P], hT[0:rows_j, P:2 * P], ALU.mult))
            step(nc.vector.tensor_tensor(hT[0:rows_j, 0:P], hT[0:rows_j, 0:P], hT[0:rows_j, P:2 * P], ALU.mult))
            dve.sem_inc(setup_dve, 1)
            dve.wait_ge(setup_pe, 1)
            nc.vector.tensor_copy(wT[:, :, :], pt[0][:, 0:3 * D].rearrange("p (w f) -> p w f", w=3)).then_inc(setup_dve, 1)
            dve.wait_ge(setup_pe, 2)
            nc.vector.tensor_reduce(scale[:, :], pt[1][:, 0:rows_j].rearrange("p (j t) -> p t j", j=JD), AXX,
                                    ALU.add).then_inc(setup_dve, 1)
            nc.vector.tensor_scalar(one_alpha[:, :], alpha_c[:, :], -1.0, 1.0, ALU.mult, ALU.add).then_inc(setup_dve, 1)
            nc.vector.tensor_scalar(alpha_acc[:, :], alpha_c[:, :], 1.0 / (A_SCALE * Y_SCALE[1]), None,
                                    ALU.mult).then_inc(setup_dve, 1)
            dve.wait_ge(setup_dve, SETUP_DVE)

            dve.wait_ge(x0_loaded, 16)
            step(nc.vector.tensor_scalar(yop[0][:, 0, :, :], x0, Y_SCALE[-1], None, ALU.mult))
            nc.vector.scalar_tensor_tensor(yop[0][:, 1, :, :], x0, Y_SCALE[-1], yop[0][:, 0, :, :],
                                           ALU.mult, ALU.subtract).then_inc(y0_ready, 1)

            def split_low(c, par, m):
                for kt in range(KT):
                    g = c * KT + kt
                    dve.wait_ge(high_done, g + 1)
                    if kt < KEPT:
                        hi = kept[:, bass.ds(c, 1), kt, 0, :].rearrange("p c n -> p (c n)")
                        lo = kept[:, bass.ds(c, 1), kt, 1, :].rearrange("p c n -> p (c n)")
                    else:
                        s = (par * UPC + (kt - KEPT) // UNIT) % 2
                        hi, lo = (stage[s][:, (kt - KEPT) % UNIT, h, :] for h in range(2))
                    nc.vector.scalar_tensor_tensor(lo, pt[kt % 4][:, :], A_SCALE, hi, ALU.mult,
                                                   ALU.subtract).then_inc(low_done, 1)
                    if kt % 8 == 2:
                        u = kt // TPC
                        dve.wait_ge(nat_loaded[u % 4], 16 * (c * 2 + u // 4 + 1))
                        nc.vector.tensor_reduce(rs_part[par][:, u, :], nat[u % 4], AXX, ALU.add
                                                ).then_inc(rows_summed_dve, 1)
                    if kt == 16 and not first(c):
                        counted(0, c - 1, lambda: epilogue(0, c - 1, 1 - par))
                dve.wait_ge(rows_summed_dve, (c + 1) * (NAT_UNITS // 2))
                dve.wait_ge(rows_summed_act, (c + 1) * (NAT_UNITS // 2))
                nc.vector.tensor_reduce(rs[:, bass.ds(c * TPC, TPC)], rs_part[par][:, :, :].rearrange("p u t -> p t u"),
                                        AXX, ALU.add).then_inc(rows_closed, 1)
            each_chunk(dve, split_low)
            counted(0, NCH - 1, lambda: epilogue(0, NCH - 1, 1))
            close(0)

            dve.wait_ge(rows_closed, NCH)
            dve.sem_inc(deg_ready, 1)
            step(nc.vector.tensor_scalar(inv_deg[:, :], rs[:, :], alpha_c[:, 0:1], one_alpha[:, 0:1], ALU.mult, ALU.add))
            step(nc.vector.tensor_scalar(zero_deg[:, :], inv_deg[:, :], 0.0, None, ALU.is_equal))
            step(nc.vector.tensor_tensor(inv_deg[:, :], inv_deg[:, :], zero_deg[:, :], ALU.add))
            step(nc.vector.reciprocal(inv_deg[:, :], inv_deg[:, :]))
            step(nc.vector.tensor_scalar(zero_deg[:, :], zero_deg[:, :], -1.0, 1.0, ALU.mult, ALU.add))
            step(nc.vector.tensor_tensor(inv_deg[:, :], inv_deg[:, :], zero_deg[:, :], ALU.mult))
            dve.wait_ge(root_ready, 1)
            step(nc.vector.reciprocal(dinv[:, :], droot[:, :]))

            def epilogues(p):
                each_chunk(dve, lambda c, par, m: counted(p, c, lambda: epilogue(p, c, par)))
                close(p)

            epilogues(1)
            epilogues(2)
            epilogues(3)

            dve.wait_ge(acc_full, nth(ALL, 3, NCH - 1))
            step(nc.vector.memset(sqT.bitcast(F32), 0.0))
            step(nc.vector.tensor_copy(ident16, ident[:, :]))
            step(nc.vector.tensor_scalar(sq_rest[:, :], sq[:, :], -0.5 * Z_SCALE * Z_SCALE, None, ALU.mult))
            for k in range(3):
                step(nc.vector.tensor_copy(sq_parts[:, :, k], sq_rest[:, :]))
                if k < 2:
                    step(nc.vector.tensor_tensor(sq_rest[:, :], sq_rest[:, :], sq_parts[:, :, k], ALU.subtract))
            dve.sem_inc(sq_ready, 1)

            search_start = count[0]

            def keep_found(i, par):
                dve.wait_ge(near_used, i + 1)
                nc.vector.tensor_copy(S[:, bass.ds(i, 1), :].rearrange("p i k -> p (i k)"), top8[par][:, 0:TOP])
                return nc.vector.tensor_copy(idx[:, bass.ds(i, 1), :].rearrange("p i k -> p (i k)"), idx8[par][:, 0:TOP])

            def search(i, par):
                dve.wait_ge(near_copied, i * NCH + NCH)
                dve.nop(nofuse=True)
                if first(i):
                    step(nc.vector.max(top8[par][:, :], near[par]))
                else:
                    nc.vector.max(top8[par][:, :], near[par]).then_inc(chain_dve, 1)
                    count[0] = i * 2 + search_start
                    step(keep_found(i - 1, 1 - par))
                dve.nop(nofuse=True)
                nc.vector.max_index(idx8[par][:, :], top8[par][:, :], near[par]).then_inc(near_used, 1)
            search(0, 0)
            search(1, 1)
            with dve.Fori(1, KT // 2) as pair:
                search(pair * 2, 0)
                search(pair * 2 + 1, 1)
            count[0] = search_start + 2 * KT - 1
            step(keep_found(KT - 1, 1))

            step(nc.vector.scalar_tensor_tensor(S[:, :, :], S[:, :, :], -2.0 / (Z_SCALE * Z_SCALE),
                                                sq[:, :].unsqueeze(2).to_broadcast([P, KT, TOP]), ALU.mult, ALU.add))
            step(nc.vector.tensor_scalar(S[:, :, :], S[:, :, :], 0.0, None, ALU.max))
            dve.sem_inc(d2_ready, 1)
            dve.wait_ge(S_ready, 2)
            step(nc.vector.tensor_reduce(droot[:, :], S[:, :, :], AXX, ALU.add))
            step(nc.vector.tensor_tensor(droot[:, :], droot[:, :], rs[:, :], ALU.add))
            dve.sem_inc(deg_ready, 1)
            dve.wait_ge(root_ready, 2)
            step(nc.vector.reciprocal(dinv2[:, :], droot[:, :]))

            dve.wait_ge(x2_loaded, 16)
            for c in range(NCH):
                y = y_all[:, c * TPC:(c + 1) * TPC, :]
                nc.vector.tensor_tensor(y, y, per_row(dinv2, c), ALU.mult).then_inc(y_scaled, 1)
            for c in range(NCH):
                dve.wait_ge(y_scaled, c + 1)
                split("y", y_all[:, c * TPC:(c + 1) * TPC, :], c)
            dve.wait_ge(late_loaded, 16 * LATE_PARAMS)
            give_indices(0, 0)
            give_indices(1, 1)
            mix(0, (0, 1, 2, 3))
            each_chunk(dve, lambda c, par, m: counted(4, c, lambda: epilogue(4, c, par)), peel_last=True)
            epilogues(5)

        def pe_turn(pe, p, c):
            if p == 3:
                pe.wait_ge(z_ready, c + 1)
                src = xout
            elif p == 4:
                pe.wait_ge(mix_ready, c + 1)
                src = mixed
            else:
                pe.wait_ge(xin_loaded, 16 * nth(XIN, p, c))
                src = xin
            if not first(c):
                if p == 3:
                    pe.wait_ge(zT_read, c)
                else:
                    pe.wait_ge(xT_ready, nth(XTS, p, c) - 1)
            elif p == 3:
                pe.wait_ge(xT_ready, nth(XTS, 2, NCH - 1))
            elif p == 4:
                pe.wait_ge(zT_read, NCH)
            elif p == 5:
                pe.wait_ge(xT_ready, nth(XTS, 4, NCH - 1))
            for t in range(TPC):
                last = nc.tensor.transpose(pxT[:, t * P:(t + 1) * P], src[:, t, :], ident[:, :])
            last.then_inc(xT_full, 1)

        def pe_project(pe, p, c):
            n = nth(ALL, p, c)
            pe.wait_ge(hT_ready, n)
            if p == 5:
                pe.wait_ge(xT_ready, nth(XTS, 5, c))
            if not (p == 0 and first(c)):
                pe.wait_ge(nat_read, n - 1)
            for t in range(TPC):
                h = hT[:, t * P:(t + 1) * P]
                if p == 1:
                    last = nc.tensor.transpose(pnat[:, t, :], h, ident[:, :])
                elif p == 5:
                    nc.tensor.matmul(pnat[:, t, :], xT[:, t * P:(t + 1) * P], wT[:, 1, :], start=True, stop=False)
                    last = nc.tensor.matmul(pnat[:, t, :], h, wT[:, 2, :], start=False, stop=True)
                else:
                    w = {0: w0_sb[:, :], 2: wT[:, 0, :], 3: wz_sb[:, :], 4: w2_sb[:, :]}[p]
                    last = nc.tensor.matmul(pnat[:, t, :], h, w, start=True, stop=True)
            last.then_inc(nat_full, 1)

        TURN_AT = {2: 2, 3: 20, 4: 18, 5: 2}
        PROJECT_AT = {0: 8, 1: 4, 2: 10, 3: 3, 4: 24, 5: 10}
        LAST_MIX_AT = (12, 16)

        def pe_epilogue_at(pe, kt, p, c):
            if TURN_AT.get(p) == kt:
                pe_turn(pe, p, c)
            if PROJECT_AT[p] == kt:
                pe_project(pe, p, c)

        def pe_epilogue(pe, p, c):
            for kt in range(KT):
                pe_epilogue_at(pe, kt, p, c)

        def products(p, par, kt, high, low):
            y = yop[OPERAND[p]]
            nc.tensor.matmul(acc[par][:, :], y[:, 0, kt, :], high, start=(kt == 0), stop=False)
            nc.tensor.matmul(acc[par][:, :], y[:, 0, kt, :], low, start=False, stop=False)
            return nc.tensor.matmul(acc[par][:, :], y[:, 1, kt, :], high, start=False, stop=(kt == KT - 1))

        @block.tensor
        def _(pe):
            pe.wait_ge(ident_made, 3)
            for loaded in par_loaded:
                pe.wait_ge(loaded, 16 * PARAMS // 2)
            for k in range(3):
                last = nc.tensor.transpose(pt[0][:, k * D:(k + 1) * D], t_nat[:, k, :], ident[:, :])
            last.then_inc(setup_pe, 1)
            pe.wait_ge(setup_dve, 1)
            rows_j = JD * KT
            nc.tensor.transpose(pt[1][:, 0:rows_j], hT[0:rows_j, 0:P], ident[0:rows_j, 0:rows_j]).then_inc(setup_pe, 1)
            pe.wait_ge(setup_dve, SETUP_DVE)

            def transposing_chunk(c, par, m):
                def products_of(kt):
                    pe.wait_ge(low_done, c * KT + kt + 1)
                    if kt < KEPT:
                        hi, lo = (kept[:, bass.ds(c, 1), kt, h, :].rearrange("p c n -> p (c n)") for h in range(2))
                    else:
                        s = (par * UPC + (kt - KEPT) // UNIT) % 2
                        hi, lo = (stage[s][:, (kt - KEPT) % UNIT, h, :] for h in range(2))
                    if first(c) and kt == 0:
                        pe.wait_ge(y0_ready, 1)
                    if kt == 0 and not among_first(c, 2):
                        pe.wait_ge(hT_ready, c - 1)
                    last = products(0, par, kt, hi, lo)
                    if kt == KT - 1:
                        last.then_inc(acc_full, 1)
                        pe.wait_ge(acc_full, c + 1)
                        pe.sem_inc(stage_used, 1)
                    elif kt >= KEPT and (kt - KEPT) % UNIT == UNIT - 1:
                        last.then_inc(stage_used, 1)

                for kt in range(KT):
                    u = kt // TPC
                    if kt % TPC == 0:
                        pe.wait_ge(nat_loaded[u % 4], 16 * (c * 2 + u // 4 + 1))
                    if not (first(c) and kt < 4):
                        pe.wait_ge(low_done, c * KT + kt - 3)
                    for t in range(TPC):
                        last = nc.tensor.transpose(pt[kt % 4][:, t * P:(t + 1) * P],
                                                   nat[u % 4][:, t, (kt % TPC) * P:(kt % TPC + 1) * P], ident[:, :])
                    last.then_inc(tr_done, 1)
                    if not first(c):
                        pe_epilogue_at(pe, kt, 0, c - 1)
                    if kt >= LAG:
                        products_of(kt - LAG)
                for kt in range(KT - LAG, KT):
                    products_of(kt)
            each_chunk(pe, transposing_chunk)

            def product_pass(p, before):
                source = "y" if p == 4 else p - 1
                def chunk(c, par, m):
                    n = nth(ALL, p, c)
                    pe.wait_ge(hT_ready, n - 2)
                    for kt in range(KT):
                        if first(c) and kt % TPC == 0:
                            pe.wait_ge(yop_ready, nth(YOP, source, kt // TPC))
                        if kt < KEPT:
                            hi, lo = (kept[:, bass.ds(c, 1), kt, h, :].rearrange("p c n -> p (c n)") for h in range(2))
                        else:
                            u = (kt - KEPT) // UNIT
                            if (kt - KEPT) % UNIT == 0:
                                pe.wait_ge(unit_loaded[u], 16 * ((p - 1) * NCH + c + 1))
                            hi, lo = (ring[u][:, (kt - KEPT) % UNIT, h, :] for h in range(2))
                        last = products(p, par, kt, hi, lo)
                        if kt == KT - 1:
                            last.then_inc(acc_full, 1)
                            pe.wait_ge(acc_full, n)
                            pe.sem_inc(unit_used, 1)
                        elif kt >= KEPT and (kt - KEPT) % UNIT == UNIT - 1:
                            last.then_inc(unit_used, 1)
                        if not first(c):
                            pe_epilogue_at(pe, kt, p, c - 1)
                        elif before == 4:
                            if kt == LAST_MIX_AT[0]:
                                pe_turn(pe, 4, NCH - 1)
                            if kt == LAST_MIX_AT[1]:
                                pe_project(pe, 4, NCH - 1)
                        elif before is not None:
                            pe_epilogue_at(pe, kt, before, NCH - 1)
                each_chunk(pe, chunk)

            product_pass(1, 0)
            product_pass(2, 1)
            product_pass(3, 2)
            pe_epilogue(pe, 3, NCH - 1)

            pe.wait_ge(sq_ready, 1)
            pe.wait_ge(hT_ready, nth(ALL, 3, NCH - 1))
            for c in range(NCH):
                if c >= 2:
                    pe.wait_ge(sqT_ready, c - 1)
                for t in range(TPC):
                    last = nc.tensor.transpose(sq_bank(c)[:, t * P:(t + 1) * P], sq_parts[:, c * TPC + t, :], ident16)
                last.then_inc(sqT_full, 1)
            pe.wait_ge(sqT_ready, NCH)
            pe.wait_ge(zT_read, NCH)

            def closeness(i):
                zh, zl = (zT[:, h, bass.ds(i * P, P)] for h in range(2))
                for j in range(NCH):
                    cols = slice(j * CHUNK, (j + 1) * CHUNK)
                    if not (first(i) and j < 4):
                        pe.wait_ge(near_copied, i * NCH + j - 3)
                    nc.tensor.matmul(pt[j % 4][:, :], zh, zT[:, 0, cols], start=True, stop=False)
                    nc.tensor.matmul(pt[j % 4][:, :], zh, zT[:, 1, cols], start=False, stop=False)
                    nc.tensor.matmul(pt[j % 4][:, :], zl, zT[:, 0, cols], start=False, stop=False)
                    nc.tensor.matmul(pt[j % 4][:, :], ones3[:, :], sqT[:, cols], start=False, stop=True
                                     ).then_inc(near_full, 1)
            closeness(0)
            with pe.Fori(1, KT) as i:
                closeness(i)

            pe.wait_ge(late_loaded, 16 * LATE_PARAMS)
            product_pass(4, None)
            product_pass(5, 4)
            pe_epilogue(pe, 5, NCH - 1)


LATE_PARAMS = 3
SETUP_DVE = 5

_INS = ["x", "adj", "L0_gnn_d_list", "L0_gnn_weight", "L0_gnn_filt", "L0_gnn_bias", "L1_gnn_alpha", "L1_gnn_W",
        "L1_gnn_b", "L2_gnn_W1", "L2_gnn_b1", "L2_gnn_W2", "L2_gnn_b2", "L3_gnn_W", "L3_gnn_b"]


def kernel(**inputs):
    import numpy as np
    import concourse.bacc as bacc
    from concourse.bass_utils import run_bass_kernel_spmd

    nc = bacc.Bacc("TRN2", target_bir_lowering=False, num_devices=1, dynamic_dma_scratch_size=4096)
    arrays, args = {}, []
    for name in _INS:
        a = np.ascontiguousarray(inputs[name])
        arrays[f"in_{name}"] = a
        args.append(nc.dram_tensor(f"in_{name}", a.shape, mybir.dt.from_np(a.dtype), kind="ExternalInput").ap())
    out = nc.dram_tensor("out_x", inputs["x"].shape, F32, kind="ExternalOutput").ap()
    gnn_kernel(nc, *args, out)
    r = run_bass_kernel_spmd(nc, [arrays], core_ids=[0])
    return r.results[0]["out_x"]
```
